# Optimizing a Trainium2 kernel written in Bass

```python
import numpy as np
import jax
import jax.numpy as jnp

def _softmax(x, axis=-1):
    return jax.nn.softmax(x, axis=axis)

def _gelu(x):
    return jax.nn.gelu(x, approximate=True)

def _silu(x):
    return jax.nn.silu(x)

def _sigmoid(x):
    return jax.nn.sigmoid(x)

def _layernorm(x, axis=-1, eps=1e-05):
    m = jnp.mean(x, axis=axis, keepdims=True)
    v = jnp.var(x, axis=axis, keepdims=True)
    return (x - m) / jnp.sqrt(v + eps)

def _scatter_add(tgt, idx, src, axis=0):
    return tgt.at[idx].add(src)

def _segment_sum(src, seg, n):
    return jax.ops.segment_sum(src, seg, n)
kernel_name = 'mk_cond_seq_d2_seqx_r2_f2e8d7'

def setup_inputs(seed: int=0):
    np.random.seed(seed)
    _w = jnp.asarray

    def _rec_inputs():
        import jax
        import jax.numpy as jnp
        _rk = jax.random.key(seed)
        x = -0.0002928 + 1 * jax.random.normal(jax.random.fold_in(_rk, 1), (64, 128, 512), jnp.float32)
        _lenS = 128 - jax.random.randint(jax.random.fold_in(_rk, 7), (64,), 0, max(1, 128 // 4) + 1, jnp.int32)
        _lenS2 = 128 - jax.random.randint(jax.random.fold_in(_rk, 8), (64,), 0, max(1, 128 // 4) + 1, jnp.int32)
        cond_2048 = 0.0061147 + 1.02565 * jax.random.normal(jax.random.fold_in(_rk, 11), (64, 1024), jnp.float32)
        _validS = jnp.arange(128)[None, :] < _lenS[:, None]
        _validS2 = jnp.arange(128)[None, :] < _lenS2[:, None]
        _causal = jnp.tril(jnp.ones((128, 128), dtype=bool))
        mask_BxS_ik0 = jnp.where(jnp.broadcast_to(_validS[:, :], (64, 128)), 0, 1).astype(jnp.int32)
        return (x, cond_2048, mask_BxS_ik0)
    x, cond_2048, mask_BxS_ik0 = _rec_inputs()

    def _L0_cond_setup():
        import jax, jax.numpy as jnp
        import numpy as np
        D = 512
        DI = 1024
        N = 16
        DT_RANK = 64
        D_CONV = 4
        EPS = 1e-05

        def _layernorm(x, g, b):
            mu = jnp.mean(x, axis=-1, keepdims=True)
            var = jnp.mean((x - mu) ** 2, axis=-1, keepdims=True)
            return (x - mu) * jax.lax.rsqrt(var + EPS) * g + b

        def _mamba(xn, in_proj_w, conv_w, conv_b, x_proj_w, dt_proj_w, dt_proj_b, A_log, D_param, out_proj_w):
            b, sl, _ = xn.shape
            xz = jnp.einsum('bsd,ed->bse', xn, in_proj_w)
            x_in, z = jnp.split(xz, 2, axis=-1)
            xt = jnp.transpose(x_in, (0, 2, 1))
            u = jax.lax.conv_general_dilated(xt, conv_w[:, None, :], (1,), [(D_CONV - 1, 0)], feature_group_count=DI, dimension_numbers=('NCH', 'OIH', 'NCH')) + conv_b[None, :, None]
            u = jax.nn.silu(jnp.transpose(u, (0, 2, 1)))
            x_dbl = jnp.einsum('bsd,ed->bse', u, x_proj_w)
            dt_r, B, C = jnp.split(x_dbl, [DT_RANK, DT_RANK + N], axis=-1)
            dt = jax.nn.softplus(jnp.einsum('bsr,dr->bsd', dt_r, dt_proj_w) + dt_proj_b)
            A = -jnp.exp(A_log)

            def step(h, inp):
                dt_t, B_t, C_t, u_t = inp
                dA = jnp.exp(dt_t[:, :, None] * A)
                h = h * dA + (dt_t * u_t)[:, :, None] * B_t[:, None, :]
                y = jnp.einsum('bdn,bn->bd', h, C_t)
                return (h, y)
            seq = (jnp.transpose(dt, (1, 0, 2)), jnp.transpose(B, (1, 0, 2)), jnp.transpose(C, (1, 0, 2)), jnp.transpose(u, (1, 0, 2)))
            h0 = jnp.zeros((b, DI, N), xn.dtype)
            _, ys = jax.lax.scan(step, h0, seq)
            y = jnp.transpose(ys, (1, 0, 2)) + u * D_param
            y = y * jax.nn.silu(z)
            return jnp.einsum('bsd,ed->bse', y, out_proj_w)
        key = jax.random.key(seed)
        ks = jax.random.split(key, 16)
        s = lambda fan: 1.0 / np.sqrt(fan)
        inp = {'x': jax.random.normal(ks[0], (2, 1024, D), jnp.float32), 'c': jax.random.normal(ks[1], (2, 2 * D), jnp.float32), 'ln_g': jnp.ones((D,), jnp.float32), 'ln_b': jnp.zeros((D,), jnp.float32), 'ada_w': jax.random.normal(ks[2], (3 * D, 2 * D), jnp.float32) * s(2 * D), 'ada_b': jnp.zeros((3 * D,), jnp.float32), 'in_proj_w': jax.random.normal(ks[3], (2 * DI, D), jnp.float32) * s(D), 'conv_w': jax.random.normal(ks[4], (DI, D_CONV), jnp.float32) * s(D_CONV), 'conv_b': jnp.zeros((DI,), jnp.float32), 'x_proj_w': jax.random.normal(ks[5], (DT_RANK + 2 * N, DI), jnp.float32) * s(DI), 'dt_proj_w': jax.random.normal(ks[6], (DI, DT_RANK), jnp.float32) * s(DT_RANK), 'dt_proj_b': jax.random.uniform(ks[7], (DI,), jnp.float32, -4.0, -2.0), 'A_log': jnp.tile(jnp.log(jnp.arange(1, N + 1, dtype=jnp.float32)), (DI, 1)), 'D_param': jnp.ones((DI,), jnp.float32), 'out_proj_w': jax.random.normal(ks[8], (D, DI), jnp.float32) * s(DI)}
        return inp
    _L0_cond_all = _L0_cond_setup()
    _L0_cond_in = {k: v for k, v in _L0_cond_all.items() if k in ('ln_g', 'ln_b', 'ada_w', 'ada_b', 'in_proj_w', 'conv_w', 'conv_b', 'x_proj_w', 'dt_proj_w', 'dt_proj_b', 'A_log', 'D_param', 'out_proj_w')}
    del _L0_cond_all

    def _L1_cond_setup():
        import jax, jax.numpy as jnp
        import numpy as np
        H = 16
        LN_EPS = 1e-05

        def _layernorm(x, scale, bias):
            mu = jnp.mean(x, axis=-1, keepdims=True)
            var = jnp.var(x, axis=-1, keepdims=True)
            return (x - mu) * jax.lax.rsqrt(var + LN_EPS) * scale + bias
        key = jax.random.key(seed)
        ks = jax.random.split(key, 8)
        B, T, D, E = (4, 2048, 512, 1024)
        s = 0.02
        return {'x': jax.random.normal(ks[0], (B, T, D), jnp.float32), 'emb': jax.random.normal(ks[1], (B, E), jnp.float32), 'src_mask': jax.random.randint(ks[2], (B, T), 0, 2).astype(jnp.int32), 'norm_scale': jnp.ones((D,), jnp.float32), 'norm_bias': jnp.zeros((D,), jnp.float32), 'Wq': jax.random.normal(ks[3], (D, D), jnp.float32) * s, 'bq': jnp.zeros((D,), jnp.float32), 'Wk': jax.random.normal(ks[4], (D, D), jnp.float32) * s, 'bk': jnp.zeros((D,), jnp.float32), 'Wv': jax.random.normal(ks[5], (D, D), jnp.float32) * s, 'bv': jnp.zeros((D,), jnp.float32), 'film_emb_W': jax.random.normal(ks[6], (E, 2 * D), jnp.float32) * s, 'film_emb_b': jnp.zeros((2 * D,), jnp.float32), 'film_norm_scale': jnp.ones((D,), jnp.float32), 'film_norm_bias': jnp.zeros((D,), jnp.float32), 'film_out_W': jax.random.normal(ks[7], (D, D), jnp.float32) * s, 'film_out_b': jnp.zeros((D,), jnp.float32)}
    _L1_cond_all = _L1_cond_setup()
    _L1_cond_in = {k: v for k, v in _L1_cond_all.items() if k in ('norm_scale', 'norm_bias', 'Wq', 'bq', 'Wk', 'bk', 'Wv', 'bv', 'film_emb_W', 'film_emb_b', 'film_norm_scale', 'film_norm_bias', 'film_out_W', 'film_out_b')}
    del _L1_cond_all
    return {'x': x, 'cond_2048': cond_2048, 'mask_BxS_ik0': mask_BxS_ik0, 'L0_cond_ln_g': _L0_cond_in['ln_g'], 'L0_cond_ln_b': _L0_cond_in['ln_b'], 'L0_cond_ada_w': _L0_cond_in['ada_w'], 'L0_cond_ada_b': _L0_cond_in['ada_b'], 'L0_cond_in_proj_w': _L0_cond_in['in_proj_w'], 'L0_cond_conv_w': _L0_cond_in['conv_w'], 'L0_cond_conv_b': _L0_cond_in['conv_b'], 'L0_cond_x_proj_w': _L0_cond_in['x_proj_w'], 'L0_cond_dt_proj_w': _L0_cond_in['dt_proj_w'], 'L0_cond_dt_proj_b': _L0_cond_in['dt_proj_b'], 'L0_cond_A_log': _L0_cond_in['A_log'], 'L0_cond_D_param': _L0_cond_in['D_param'], 'L0_cond_out_proj_w': _L0_cond_in['out_proj_w'], 'L1_cond_norm_scale': _L1_cond_in['norm_scale'], 'L1_cond_norm_bias': _L1_cond_in['norm_bias'], 'L1_cond_Wq': _L1_cond_in['Wq'], 'L1_cond_bq': _L1_cond_in['bq'], 'L1_cond_Wk': _L1_cond_in['Wk'], 'L1_cond_bk': _L1_cond_in['bk'], 'L1_cond_Wv': _L1_cond_in['Wv'], 'L1_cond_bv': _L1_cond_in['bv'], 'L1_cond_film_emb_W': _L1_cond_in['film_emb_W'], 'L1_cond_film_emb_b': _L1_cond_in['film_emb_b'], 'L1_cond_film_norm_scale': _L1_cond_in['film_norm_scale'], 'L1_cond_film_norm_bias': _L1_cond_in['film_norm_bias'], 'L1_cond_film_out_W': _L1_cond_in['film_out_W'], 'L1_cond_film_out_b': _L1_cond_in['film_out_b']}

def reference(x, cond_2048, mask_BxS_ik0, L0_cond_ln_g, L0_cond_ln_b, L0_cond_ada_w, L0_cond_ada_b, L0_cond_in_proj_w, L0_cond_conv_w, L0_cond_conv_b, L0_cond_x_proj_w, L0_cond_dt_proj_w, L0_cond_dt_proj_b, L0_cond_A_log, L0_cond_D_param, L0_cond_out_proj_w, L1_cond_norm_scale, L1_cond_norm_bias, L1_cond_Wq, L1_cond_bq, L1_cond_Wk, L1_cond_bk, L1_cond_Wv, L1_cond_bv, L1_cond_film_emb_W, L1_cond_film_emb_b, L1_cond_film_norm_scale, L1_cond_film_norm_bias, L1_cond_film_out_W, L1_cond_film_out_b):
    import jax
    import jax.numpy as jnp

    def _L0_cond_ref(x, c, ln_g, ln_b, ada_w, ada_b, in_proj_w, conv_w, conv_b, x_proj_w, dt_proj_w, dt_proj_b, A_log, D_param, out_proj_w):
        import jax, jax.numpy as jnp
        import numpy as np
        D = 512
        DI = 1024
        N = 16
        DT_RANK = 64
        D_CONV = 4
        EPS = 1e-05

        def _layernorm(x, g, b):
            mu = jnp.mean(x, axis=-1, keepdims=True)
            var = jnp.mean((x - mu) ** 2, axis=-1, keepdims=True)
            return (x - mu) * jax.lax.rsqrt(var + EPS) * g + b

        def _mamba(xn, in_proj_w, conv_w, conv_b, x_proj_w, dt_proj_w, dt_proj_b, A_log, D_param, out_proj_w):
            b, sl, _ = xn.shape
            xz = jnp.einsum('bsd,ed->bse', xn, in_proj_w)
            x_in, z = jnp.split(xz, 2, axis=-1)
            xt = jnp.transpose(x_in, (0, 2, 1))
            u = jax.lax.conv_general_dilated(xt, conv_w[:, None, :], (1,), [(D_CONV - 1, 0)], feature_group_count=DI, dimension_numbers=('NCH', 'OIH', 'NCH')) + conv_b[None, :, None]
            u = jax.nn.silu(jnp.transpose(u, (0, 2, 1)))
            x_dbl = jnp.einsum('bsd,ed->bse', u, x_proj_w)
            dt_r, B, C = jnp.split(x_dbl, [DT_RANK, DT_RANK + N], axis=-1)
            dt = jax.nn.softplus(jnp.einsum('bsr,dr->bsd', dt_r, dt_proj_w) + dt_proj_b)
            A = -jnp.exp(A_log)

            def step(h, inp):
                dt_t, B_t, C_t, u_t = inp
                dA = jnp.exp(dt_t[:, :, None] * A)
                h = h * dA + (dt_t * u_t)[:, :, None] * B_t[:, None, :]
                y = jnp.einsum('bdn,bn->bd', h, C_t)
                return (h, y)
            seq = (jnp.transpose(dt, (1, 0, 2)), jnp.transpose(B, (1, 0, 2)), jnp.transpose(C, (1, 0, 2)), jnp.transpose(u, (1, 0, 2)))
            h0 = jnp.zeros((b, DI, N), xn.dtype)
            _, ys = jax.lax.scan(step, h0, seq)
            y = jnp.transpose(ys, (1, 0, 2)) + u * D_param
            y = y * jax.nn.silu(z)
            return jnp.einsum('bsd,ed->bse', y, out_proj_w)
        ada = jnp.einsum('bc,ec->be', jax.nn.silu(c), ada_w) + ada_b
        shift, scale, gate = jnp.split(ada, 3, axis=1)
        xn = _layernorm(x, ln_g, ln_b)
        xn = xn * (1.0 + scale[:, None, :]) + shift[:, None, :]
        x_ssm = _mamba(xn, in_proj_w, conv_w, conv_b, x_proj_w, dt_proj_w, dt_proj_b, A_log, D_param, out_proj_w)
        return x + gate[:, None, :] * x_ssm

    def _L1_cond_ref(x, emb, src_mask, norm_scale, norm_bias, Wq, bq, Wk, bk, Wv, bv, film_emb_W, film_emb_b, film_norm_scale, film_norm_bias, film_out_W, film_out_b):
        import jax, jax.numpy as jnp
        import numpy as np
        H = 16
        LN_EPS = 1e-05

        def _layernorm(x, scale, bias):
            mu = jnp.mean(x, axis=-1, keepdims=True)
            var = jnp.var(x, axis=-1, keepdims=True)
            return (x - mu) * jax.lax.rsqrt(var + LN_EPS) * scale + bias
        B, T, D = x.shape
        dh = D // H
        xn = _layernorm(x, norm_scale, norm_bias)
        q = xn @ Wq + bq
        k = xn @ Wk + bk
        v = xn @ Wv + bv
        mask = (src_mask == 1)[:, :, None]
        k = jnp.where(mask, -jnp.inf, k)
        v = jnp.where(mask, 0.0, v)
        q = q.reshape(B, T, H, dh).transpose(0, 2, 1, 3)
        k = k.reshape(B, T, H, dh).transpose(0, 2, 1, 3)
        v = v.reshape(B, T, H, dh).transpose(0, 2, 1, 3)
        q = jax.nn.softmax(q, axis=-1)
        k = jax.nn.softmax(k, axis=2)
        attn = jnp.einsum('bhse,bhsd->bhed', k, v)
        y = jnp.einsum('bhtd,bhed->bhte', q, attn)
        y = y.transpose(0, 2, 1, 3).reshape(B, T, D)
        emb_out = jax.nn.silu(emb) @ film_emb_W + film_emb_b
        scale, shift = jnp.split(emb_out, 2, axis=-1)
        h = _layernorm(y, film_norm_scale, film_norm_bias) * (1.0 + scale[:, None, :]) + shift[:, None, :]
        h = jax.nn.silu(h) @ film_out_W + film_out_b
        return x + h
    x = _L0_cond_ref(x, cond_2048, L0_cond_ln_g, L0_cond_ln_b, L0_cond_ada_w, L0_cond_ada_b, L0_cond_in_proj_w, L0_cond_conv_w, L0_cond_conv_b, L0_cond_x_proj_w, L0_cond_dt_proj_w, L0_cond_dt_proj_b, L0_cond_A_log, L0_cond_D_param, L0_cond_out_proj_w)
    x = _L1_cond_ref(x, cond_2048, mask_BxS_ik0, L1_cond_norm_scale, L1_cond_norm_bias, L1_cond_Wq, L1_cond_bq, L1_cond_Wk, L1_cond_bk, L1_cond_Wv, L1_cond_bv, L1_cond_film_emb_W, L1_cond_film_emb_b, L1_cond_film_norm_scale, L1_cond_film_norm_bias, L1_cond_film_out_W, L1_cond_film_out_b)
    return x

_drawn_inputs = setup_inputs


def setup_inputs(seed=0):
    import zlib

    import numpy as np

    out = dict(_drawn_inputs(seed))
    spreads = {'L0_cond_ln_g': (1.0, 0.2),
     'L0_cond_ln_b': (0.0, 0.1),
     'L0_cond_ada_b': (0.0, 0.1),
     'L0_cond_conv_b': (0.0, 0.1),
     'L0_cond_D_param': (1.0, 0.2),
     'L1_cond_norm_scale': (1.0, 0.2),
     'L1_cond_norm_bias': (0.0, 0.1),
     'L1_cond_bq': (0.0, 0.372),
     'L1_cond_bk': (0.0, 0.8),
     'L1_cond_bv': (0.0, 0.1),
     'L1_cond_film_emb_b': (0.0, 0.1),
     'L1_cond_film_norm_scale': (1.0, 0.2),
     'L1_cond_film_norm_bias': (0.0, 0.296),
     'L1_cond_film_out_b': (0.0, 0.1)}
    factors = {}
    for name, (base, spread) in spreads.items():
        noise = np.random.default_rng([zlib.crc32(name.encode()), seed]).standard_normal(out[name].shape)
        drawn = base * np.exp(spread * noise) if base else spread * noise
        out[name] = jnp.asarray(drawn.astype(out[name].dtype))
    for name, factor in factors.items():
        out[name] = (out[name] * factor).astype(out[name].dtype)
    return out
```

```python
from contextlib import ExitStack

import concourse.bass as bass
from concourse import mybir

F32 = mybir.dt.float32
I32 = mybir.dt.int32
ALU = mybir.AluOpType
ACT = mybir.ActivationFunctionType
AX = mybir.AxisListType

P = 128
D = 512
DI = 1024
NST = 16
RANK = 64
TAPS = 4
COND = 1024
HD = 32
EPS = 1e-5
KD = D // P
KI = DI // P
GB = 2
GT = GB * P
QUARTERS = NST * 4


def wait(eng, sem, value):
    if isinstance(value, int) and value <= 0:
        return
    eng.wait_ge(sem, value)


def sp_wait(sp, sem, value):
    wait(sp, sem, value)
    sp.nop(nofuse=True)


SIDE = [
    ("Z", 0), ("Z", 1), ("Z", 2), ("Z", 3),
    ("XN", 0), ("YT", 0), ("XN", 1), ("YT", 1),
    ("XI", 0), ("YT", 2), ("XI", 1), ("YT", 3),
    ("XI", 2), ("O", 0), ("XI", 3), ("O", 1),
    ("CV", 0), ("CV", 1), ("CV", 2), ("UT", 0), ("CV", 3), ("UT", 1),
    ("XP", 0), ("UT", 2), ("BC", 0), ("UT", 3),
    ("DT", 0), ("DT", 1), ("DT", 2), ("DT", 3),
]
POST = ("Z", "YT", "O")
N_POST = sum(kind in POST for kind, _ in SIDE)
N_PRE = len(SIDE) - N_POST
SIGS = ("Z", "CV", "DT")
UT_BLOCK = [(0, 0), (1, 0), (0, 1), (1, 1)]
Z_BLOCK = [(0, 0), (0, 1), (1, 0), (1, 1)]


def start_at(c):
    return 2 * c + 1


def side_of(post, pre):
    some = [(kind, j, start_at(c)) for c, (kind, j) in enumerate(SIDE) if (post if kind in POST else pre)]
    return [(kind, j, at, c) for c, (kind, j, at) in enumerate(some)]


def mamba(nc, ctx, NG, W, C, io):

    def sb(name, shape, dt=F32):
        return ctx.enter_context(nc.sbuf_tensor(name, shape, dt))

    def sem(name):
        return ctx.enter_context(nc.semaphore(name))

    x_in = sb("x_in", [P, GB, D])
    xhat = sb("xhat", [P, GB, D])
    stats = sb("stats", [P, GB, 6])
    mv = sb("mv", [P, GB, 2])
    lnv = sb("lnv", [P, GB])
    rstd = sb("rstd", [P, GB])
    xnF = [sb(f"xnF{i}", [P, KD, GT]) for i in range(2)]
    xin = sb("xin", [P, KI, GB, TAPS - 1 + P])
    u = [sb(f"u{i}", [P, KI, GT]) for i in range(2)]
    yzF = [a[:, :, :].rearrange("p k (b t) -> p k b t", b=GB) for a in u]
    tmp = [sb(f"tmp{i}", [P, D]) for i in range(2)]
    dtr = sb("dtr", [RANK + 1, GT])
    dt = [sb(f"dt{i}", [P, KI, GT]) for i in range(2)]
    brow = sb("brow", [RANK + NST, GT])
    bbc = sb("bbc", [P, NST, GT])
    acc = [sb(f"acc{i}", [P, GB, DI]) for i in range(2)]
    ct = [sb(f"ct{i}", [P, GB, NST]) for i in range(2)]
    dbu = [sb(f"dbu{i}", [P, 2, GT]) for i in range(4)]
    h = [sb(f"h{i}", [P, D]) for i in range(4)]
    gb = sb("gb", [P, GB, D])
    xres = sb("xres", [P, GB, D])

    bank = [ctx.enter_context(nc.psum_tensor(f"side{i}", [P, 512], F32)) for i in range(2)]
    dA = [ctx.enter_context(nc.psum_tensor(f"dA{i}", [P, 2, GB, P], F32)) for i in range(2)]
    hT = [[ctx.enter_context(nc.psum_tensor(f"hT{i}{b}", [P, 512], F32)) for b in range(GB)] for i in range(2)]

    x_loaded, xres_loaded, gate_loaded, x1_stored = (sem(n) for n in ("x_loaded", "xres_loaded", "gate_loaded", "x1_stored"))
    init_done, dA_ready, dbu_ready, scan_done, ht_filled, c_dve, b_stored = (
        sem(n) for n in ("init_done", "dA_ready", "dbu_ready", "scan_done", "ht_filled", "c_dve", "b_stored"))
    b_loaded = [sem(f"b_loaded{k}") for k in range(4)]
    bn_done, stats_done, lnv_done, rstd_done, xhat_done, filled, act_step, sig_ready = (
        sem(n) for n in ("bn_done", "stats_done", "lnv_done", "rstd_done", "xhat_done", "filled", "act_step", "sig_ready"))
    xn_done, xin_done, u_done, brow_done, dtr_done, bc_done, dt_done, acc_init, du_done = (
        sem(n) for n in ("xn_done", "xin_done", "u_done", "brow_done", "dtr_done", "bc_done", "dt_done", "acc_init", "du_done"))
    zs_done, yz_done, yzf_done, og_done, x1_done = (sem(n) for n in ("zs_done", "yz_done", "yzf_done", "og_done", "x1_done"))

    def before(g, n_pre, n_post):
        if isinstance(g, int):
            return n_pre * min(g + 1, NG) + n_post * max(g - 1, 0)
        return g * (n_pre + n_post) + (n_pre - n_post)

    def emptied(kind, j, gp, gq):
        s, n, g = {
            "Z": (zs_done, 4, gq), "YT": (yzf_done, 4, gq), "O": (og_done, 2, gq), "XN": (xn_done, 2, gp),
            "XI": (xin_done, 4, gp), "CV": (u_done, 4, gp), "XP": (dtr_done, 1, gp), "BC": (bc_done, 1, gp),
            "DT": (dt_done, 4, gp), "UT": (acc_init, 4, gp)}[kind]
        return s, g * n + (j + 1)

    def over_groups(eng, body):
        body(-1, 1, False, False, True)
        body(0, 0, True, False, True)
        with eng.Fori(0, (NG - 2) // 2) as i:
            body(i * 2 + 1, 1, True, True, True)
            body(i * 2 + 2, 0, True, True, True)
        body(NG - 1, (NG - 1) % 2, True, True, False)
        body(NG, NG % 2, False, True, False)

    def scanned_half(g, q, scan, post):
        if q % 2 == 0:
            return None
        if q >= 3:
            return (g, (q - 3) // 2) if scan else None
        return (g - 1, QUARTERS // 2 - 1) if post else None

    block = ctx.enter_context(nc.Block())

    @block.sync
    def _(sp):
        def body(g, par, scan, post, pre):
            gp, gq = g + 1, g - 1
            if pre:
                sp_wait(sp, xhat_done, gp * GB)
                sp.dma_start(x_in[:, :, :], io["x"][bass.ds(gp * GB, GB), :, :].rearrange("b t d -> t b d")).then_inc(x_loaded, 16)
            if scan:
                sp_wait(sp, dbu_ready, g * QUARTERS)
                sp.dma_start(bbc[:, 12:16, :], io["b"][12:16, :].partition_broadcast(P)).then_inc(b_loaded[3], 16)
            if post:
                sp.dma_start(xres[:, :, :], io["x"][bass.ds(gq * GB, GB), :, :].rearrange("b t d -> t b d")).then_inc(xres_loaded, 16)
                sp.dma_start(gb[:, :, :], io["gate"][bass.ds(gq * GB, GB), :].partition_broadcast(P)).then_inc(gate_loaded, 16)
                sp_wait(sp, x1_done, gq * GB + GB)
                sp.dma_start(io["x1"][bass.ds(gq * GB, GB), :, :].rearrange("b t d -> t b d"), xres[:, :, :]).then_inc(x1_stored, 16)
            if pre:
                sp_wait(sp, b_loaded[3], 16 * gp)
                sp_wait(sp, brow_done, gp + 1)
                sp.dma_start(io["b"], brow[RANK:RANK + NST, :]).then_inc(b_stored, 16)
                sp_wait(sp, b_stored, 16 * gp + 16)
                for k in range(3):
                    if scan:
                        sp_wait(sp, dbu_ready, g * QUARTERS + 16 * (k + 1))
                    sp.dma_start(bbc[:, 4 * k:4 * k + 4, :], io["b"][4 * k:4 * k + 4, :].partition_broadcast(P)).then_inc(b_loaded[k], 16)
            if post:
                sp_wait(sp, x1_stored, gq * 16 + 16)

        over_groups(sp, body)
        sp.wait_ge(x1_stored, 16 * NG)

    @block.tensor
    def _(pe):
        def fill_ht(g, q):
            half, n = (q // 2) % 2, q // 4
            wait(pe, scan_done, g * QUARTERS + (q + 1))
            if q % 2 == 0:
                wait(pe, c_dve, g * QUARTERS + (4 * n if half else 4 * n - 2))
            for e in range(2):
                for b in range(GB):
                    dst = ((q % 2) * 2 + e) * P
                    last = pe.transpose(hT[half][b][:, dst:dst + P],
                                        h[q % 4][:, (e * GB + b) * P:(e * GB + b + 1) * P], C["ident"][:, :])
            last.then_inc(ht_filled, 1)

        def piece(kind, j, c, part, gp, gq, par):
            nxt = 1 - par
            out = bank[c % 2]
            if kind == "Z":
                b, hf = Z_BLOCK[j]
                for k in (0, 1) if part == 0 else (2, 3):
                    last = pe.matmul(out[:, :], xnF[nxt][:, k, b * P:(b + 1) * P],
                                     W["in"][:, k, DI + hf * D:DI + (hf + 1) * D], start=(k == 0), stop=(k == 3))
            elif kind == "YT":
                b, hf = Z_BLOCK[j]
                if part == 0:
                    wait(pe, yz_done, gq * 4 + (j + 1))
                for k in (0, 1) if part == 0 else (2, 3):
                    s = hf * D + k * P
                    last = pe.transpose(out[:, k * P:(k + 1) * P], acc[nxt][:, b, s:s + P], C["ident"][:, :])
            elif kind == "O":
                if part == 0:
                    wait(pe, yzf_done, gq * 4 + 2 * (j + 1))
                for k in range(0, 4) if part == 0 else range(4, 8):
                    last = pe.matmul(out[:, :], yzF[nxt][:, k, j, :], W["out"][:, k, :], start=(k == 0), stop=(k == 7))
            elif kind == "XN":
                if part == 0:
                    wait(pe, xhat_done, gp * GB + GB)
                k = 2 * j + part
                for b in range(GB):
                    s = (part * GB + b) * P
                    last = pe.transpose(out[:, s:s + P], xhat[:, b, k * P:(k + 1) * P], C["ident"][:, :])
            elif kind == "XI":
                if part == 0:
                    wait(pe, xn_done, gp * 2 + 2)
                e = 2 * j + part
                for k in range(KD):
                    last = pe.matmul(out[:, part * GT:(part + 1) * GT], W["in"][:, k, e * P:(e + 1) * P],
                                     xnF[nxt][:, k, :], start=(k == 0), stop=(k == 3))
            elif kind == "CV":
                if part == 0:
                    wait(pe, xin_done, gp * 4 + (j + 1))
                e = 2 * j + part
                for t in range(TAPS):
                    last = pe.matmul(out[:, part * GT:(part + 1) * GT].rearrange("p (b t) -> p b t", b=GB),
                                     W["conv"][:, e, t, :], xin[:, e, :, t:t + P], start=(t == 0), stop=(t == 3))
            elif kind == "XP":
                if part == 0:
                    wait(pe, u_done, gp * 4 + 4)
                for k in range(0, 4) if part == 0 else range(4, 8):
                    last = pe.matmul(out[0:RANK + NST, 0:GT], W["x"][:, k, 0:RANK + NST], u[nxt][:, k, :], start=(k == 0), stop=(k == 7))
            elif kind == "BC":
                for k in range(KI):
                    last = pe.matmul(out[:, part * NST:(part + 1) * NST], u[nxt][:, k, part * P:(part + 1) * P],
                                     W["x"][:, k, RANK + NST:RANK + 2 * NST], start=(k == 0), stop=(k == 7))
            elif kind == "DT":
                if part == 0:
                    wait(pe, dtr_done, gp + 1)
                e = 2 * j + part
                last = pe.matmul(out[:, part * GT:(part + 1) * GT], W["dt"][:, e * P:(e + 1) * P], dtr[:, :],
                                 start=True, stop=True)
            elif kind == "UT":
                b, hf = UT_BLOCK[j]
                if part == 0:
                    wait(pe, u_done, gp * 4 + 2 * (hf + 1))
                for k in (0, 1) if part == 0 else (2, 3):
                    last = pe.transpose(out[:, k * P:(k + 1) * P], u[nxt][:, hf * 4 + k, b * P:(b + 1) * P], C["ident"][:, :])
            if part == 1:
                last.then_inc(filled, 1)

        def body(g, par, scan, post, pre):
            gp, gq = g + 1, g - 1
            side = side_of(post, pre)
            for q in range(QUARTERS):
                if q >= 2 and scan:
                    fill_ht(g, q - 2)
                if q < 2 and post:
                    fill_ht(g - 1, QUARTERS - 2 + q)
                for kind, j, at, c in side:
                    if q == at:
                        if c >= 2:
                            wait(pe, *emptied(side[c - 2][0], side[c - 2][1], gp, gq))
                        elif isinstance(g, int) and g == NG:
                            wait(pe, *emptied("O", c, gp, gq - 1))
                        else:
                            wait(pe, *emptied("DT", 2 + c, g, gq))
                        piece(kind, j, c, 0, gp, gq, par)
                    if q == at + 1:
                        piece(kind, j, c, 1, gp, gq, par)

        pe.wait_ge(init_done, 4)
        over_groups(pe, body)

    @block.scalar
    def _(act):
        act.preload_act_table_set("natural_log_exp_and_others")
        act.wait_ge(init_done, 4)

        def decay(g, q, e, par):
            k, n = 2 * (q % 4) + e, q // 4
            last = act.activation(dA[q % 2][:, e, :, 1:P], dt[par][:, k, :].rearrange("p (b t) -> p b t", b=GB)[:, :, 1:P],
                                  ACT.Exp, scale=C["A"][:, k, n:n + 1])
            if e == 1:
                last.then_inc(dA_ready, 1)

        def simple(kind, j, c, g, gp, gq, par):
            nxt = 1 - par
            src = bank[c % 2]
            wait(act, filled, before(g, N_PRE, N_POST) + (c + 1))
            if kind == "XN":
                for part in range(2):
                    for b in range(GB):
                        k, s = 2 * j + part, (part * GB + b) * P
                        last = act.activation(xnF[nxt][:, k, b * P:(b + 1) * P], src[:, s:s + P], ACT.Identity,
                                              scale=C["gm0"][:, bass.ds(gp * GB + b, 1), k], bias=C["bm0"][:, bass.ds(gp * GB + b, 1), k])
                last.then_inc(xn_done, 1)
            elif kind == "XI":
                act.activation(xin[:, 2 * j:2 * j + 2, :, TAPS - 1:].rearrange("p e b t -> p (e b) t"),
                               src[:, :].rearrange("p (e b t) -> p (e b) t", e=2, b=GB), ACT.Copy).then_inc(xin_done, 1)
            elif kind == "XP":
                wait(act, b_stored, 16 * gp)
                act.activation(brow[RANK:RANK + NST, :], src[RANK:RANK + NST, 0:GT], ACT.Copy).then_inc(brow_done, 1)
                act.activation(dtr[0:RANK, :], src[0:RANK, 0:GT], ACT.Copy).then_inc(dtr_done, 1)
            elif kind == "YT":
                b, hf = Z_BLOCK[j]
                act.activation(yzF[nxt][:, 4 * hf:4 * hf + 4, b, :], src[:, :].rearrange("p (k t) -> p k t", k=4),
                               ACT.Copy).then_inc(yzf_done, 1)

        def staged(kind, j, c, stage, sig, zs_before, g, gq, post):
            src, t = bank[c % 2], tmp[c % 2]
            step = before(g, 16, 8) + 2 * sig
            if stage == 0:
                wait(act, filled, before(g, N_PRE, N_POST) + (c + 1))
                if post and zs_before:
                    wait(act, yz_done, gq * 4 + zs_before)
                if kind == "Z":
                    act.activation(t[:, :], src[:, :], ACT.Exp, scale=-1.0).then_inc(act_step, 1)
                elif kind == "CV":
                    for e in range(2):
                        last = act.activation(t[:, e * GT:(e + 1) * GT], src[:, e * GT:(e + 1) * GT], ACT.Exp, scale=-1.0,
                                              bias=C["ncb"][:, 2 * j + e:2 * j + e + 1])
                    last.then_inc(act_step, 1)
                else:
                    act.activation(t[:, :], src[:, :], ACT.Abs).then_inc(act_step, 1)
            elif stage == 1:
                wait(act, act_step, step + 1)
                if kind == "DT":
                    act.activation(t[:, :], t[:, :], ACT.Exp, scale=-1.0).then_inc(act_step, 1)
                else:
                    act.activation(t[:, :], t[:, :], ACT.Ln, bias=1.0).then_inc(act_step, 1)
            else:
                wait(act, act_step, step + 2)
                if kind == "DT":
                    act.activation(t[:, :], t[:, :], ACT.Ln, bias=1.0).then_inc(sig_ready, 1)
                else:
                    act.activation(t[:, :], t[:, :], ACT.Exp, scale=-1.0).then_inc(sig_ready, 1)

        def body(g, par, scan, post, pre):
            gp, gq = g + 1, g - 1
            side = side_of(post, pre)
            sig_of = {c: i for i, c in enumerate(c for kind, _, _, c in side if kind in SIGS)}

            def stages(q, stage, at_offset):
                for kind, j, at, c in side:
                    if kind in SIGS and q == at + at_offset:
                        zs = sum(k2 == "Z" for k2, _, _, c2 in side if c2 <= c - 2)
                        staged(kind, j, c, stage, sig_of[c], zs, g, gq, post)

            for q in range(QUARTERS):
                if scan:
                    wait(act, scan_done, g * QUARTERS + (q - 1))
                    if q < 4:
                        wait(act, dt_done, g * 4 + (q + 1))
                    decay(g, q, 0, par)
                stages(q, 1, 2)
                if scan:
                    decay(g, q, 1, par)
                stages(q, 2, 2)
                stages(q, 0, 1)
                for kind, j, at, c in side:
                    if q == at + 1 and kind in ("XN", "XI", "XP", "YT"):
                        simple(kind, j, c, g, gp, gq, par)
                if pre and q == 4:
                    wait(act, stats_done, gp + 1)
                    act.activation(lnv[:, :], mv[:, :, 1], ACT.Ln, bias=C["eps"][:, 0:1]).then_inc(lnv_done, 1)
                    wait(act, lnv_done, gp + 1)
                    act.activation(rstd[:, :], lnv[:, :], ACT.Exp, scale=-0.5).then_inc(rstd_done, 1)

        over_groups(act, body)

    @block.vector
    def _(dve):
        for i in range(2):
            dve.memset(dA[i][:, :, :, 0:1], 0.0).then_inc(init_done, 1)
        dve.memset(xin[:, :, :, 0:TAPS - 1], 0.0).then_inc(init_done, 1)
        dve.memset(dtr[RANK:RANK + 1, :], 1.0).then_inc(init_done, 1)
        dve.wait_ge(init_done, 4)

        def add_c(g, half, par):
            n, hf = half // 2, half % 2
            wait(dve, ht_filled, g * QUARTERS + 2 * (half + 1))
            if n == 0:
                wait(dve, acc_init, g * 4 + 4)
                wait(dve, bc_done, g + 1)
            for b in range(GB):
                idx = 2 * hf + b
                if n:
                    wait(dve, c_dve, g * QUARTERS + (4 * (n - 1) + idx + 1))
                blk = acc[par][:, b, hf * D:(hf + 1) * D]
                dve.scalar_tensor_tensor(blk, hT[hf][b][:, :], ct[par][:, b, n:n + 1], blk,
                                         ALU.mult, ALU.add).then_inc(c_dve, 1)

        def side_dve(kind, j, c, sig, g, gp, gq, par):
            nxt = 1 - par
            src, t = bank[c % 2], tmp[c % 2]
            if kind in SIGS:
                wait(dve, sig_ready, before(g, 8, 4) + (sig + 1))
            else:
                wait(dve, filled, before(g, N_PRE, N_POST) + (c + 1))
            if kind == "Z":
                b, hf = Z_BLOCK[j]
                dve.tensor_tensor(t[:, :], src[:, :], t[:, :], ALU.mult).then_inc(zs_done, 1)
                wait(dve, c_dve, gq * QUARTERS + QUARTERS)
                wait(dve, zs_done, gq * 4 + (j + 1))
                blk = acc[nxt][:, b, hf * D:(hf + 1) * D]
                dve.tensor_tensor(blk, blk, t[:, :], ALU.mult).then_inc(yz_done, 1)
            elif kind == "O":
                wait(dve, gate_loaded, gq * 16 + 16)
                dve.tensor_tensor(gb[:, j, :], src[:, :], gb[:, j, :], ALU.mult).then_inc(og_done, 1)
            elif kind == "CV":
                for e in range(2):
                    last = dve.scalar_tensor_tensor(u[nxt][:, 2 * j + e, :], src[:, e * GT:(e + 1) * GT],
                                                    C["cb"][:, 2 * j + e:2 * j + e + 1], t[:, e * GT:(e + 1) * GT],
                                                    ALU.add, ALU.mult)
                last.then_inc(u_done, 1)
            elif kind == "BC":
                wait(dve, c_dve, g * QUARTERS)
                dve.tensor_copy(ct[nxt][:, :, :], src[:, 0:GB * NST].rearrange("p (b n) -> p b n", b=GB)).then_inc(bc_done, 1)
            elif kind == "DT":
                wait(dve, dA_ready, g * QUARTERS)
                dve.scalar_tensor_tensor(dt[nxt][:, 2 * j:2 * j + 2, :].rearrange("p e t -> p (e t)"), src[:, :], 0.0, t[:, :],
                                         ALU.max, ALU.add).then_inc(dt_done, 1)
                if j % 2 == 1:
                    hf = j // 2
                    wait(dve, dt_done, gp * 4 + (j + 1))
                    for k in (4 * hf, 4 * hf + 2):
                        last = dve.tensor_tensor(u[nxt][:, k:k + 2, :], dt[nxt][:, k:k + 2, :], u[nxt][:, k:k + 2, :], ALU.mult)
                    last.then_inc(du_done, 1)
            elif kind == "UT":
                b, hf = UT_BLOCK[j]
                dve.tensor_tensor(acc[nxt][:, b, hf * D:(hf + 1) * D], src[:, :], C["dbc"][:, hf * D:(hf + 1) * D],
                                  ALU.mult).then_inc(acc_init, 1)

        def body(g, par, scan, post, pre):
            gp, gq = g + 1, g - 1
            side = side_of(post, pre)
            sig_of = {c: i for i, c in enumerate(c for kind, _, _, c in side if kind in SIGS)}
            for q in range(QUARTERS):
                if pre and q == 3:
                    wait(dve, bn_done, gp * GB + GB)
                if scan:
                    wait(dve, dA_ready, g * QUARTERS + (q + 1))
                    wait(dve, dbu_ready, g * QUARTERS + (q + 1))
                    wait(dve, ht_filled, g * QUARTERS + (q - 3))
                    dve.tensor_tensor_scan(h[q % 4][:, :], dA[q % 2][:, :, :, :].rearrange("p e b t -> p (e b t)"),
                                           dbu[q % 4][:, :, :].rearrange("p e t -> p (e t)"), 0.0, ALU.mult, ALU.add).then_inc(scan_done, 1)
                done = scanned_half(g, q, scan, post)
                if done:
                    add_c(done[0], done[1], par if q >= 3 else 1 - par)
                if pre and q == 2:
                    wait(dve, x_loaded, gp * 16 + 16)
                    for b in range(GB):
                        dve.bn_stats(stats[:, b, :], x_in[:, b, :]).then_inc(bn_done, 1)
                if pre and q == 3:
                    for b in range(GB):
                        last = dve.bn_aggr(mv[:, b, :], stats[:, b, :])
                    last.then_inc(stats_done, 1)
                if pre and q == 6:
                    wait(dve, rstd_done, gp + 1)
                    for b in range(GB):
                        dve.tensor_scalar(xhat[:, b, :], x_in[:, b, :], mv[:, b, 0:1], rstd[:, b:b + 1],
                                          ALU.subtract, ALU.mult).then_inc(xhat_done, 1)
                for kind, j, at, c in side:
                    if (kind in SIGS and q == at + 3) or (kind in ("O", "BC", "UT") and q == at + 2):
                        side_dve(kind, j, c, sig_of.get(c), g, gp, gq, par)

        over_groups(dve, body)

    @block.gpsimd
    def _(gps):
        def scale_b(g, q, par):
            n, k = q // 4, 2 * (q % 4)
            wait(gps, scan_done, g * QUARTERS + (q - 3))
            if q % 16 == 0:
                wait(gps, b_loaded[q // 16], g * 16 + 16)
            if q < 4:
                wait(gps, du_done, g * 2 + (q // 2 + 1))
            gps.tensor_tensor(dbu[q % 4][:, :, :], u[par][:, k:k + 2, :], bbc[:, n:n + 1, :].broadcast_to([P, 2, GT]),
                              ALU.mult).then_inc(dbu_ready, 1)

        def body(g, par, scan, post, pre):
            gq = g - 1
            side = side_of(post, pre)
            for q in range(QUARTERS):
                if scan:
                    scale_b(g, q, par)
                for kind, j, at, c in side:
                    if kind == "O" and q == at + 4:
                        wait(gps, og_done, gq * GB + (j + 1))
                        wait(gps, xres_loaded, gq * 16 + 16)
                        gps.tensor_tensor(xres[:, j, :], xres[:, j, :], gb[:, j, :], ALU.add).then_inc(x1_done, 1)

        over_groups(gps, body)


def attention(nc, ctx, NG, C, io):

    def sb(name, shape, dt=F32):
        return ctx.enter_context(nc.sbuf_tensor("p3_" + name, shape, dt))

    def sem(name):
        return ctx.enter_context(nc.semaphore(name))

    MASKED = -3.0e38
    NH = D // HD
    wk, wv, wq, wo = (sb(n, [P, KD, D]) for n in ("wk", "wv", "wq", "wo"))
    bv, bq, bo = (sb(n, [P, D]) for n in ("bv_all", "bq_all", "bo_all"))
    cols = sb("ncols", [P, 3, KD])
    heads = sb("heads", [P, P])
    x_in = sb("x1_in", [P, GB, D])
    stats = sb("stats1", [P, GB, 6])
    mv = sb("mv1", [P, GB, 2])
    rstd = sb("rstd1", [P, 2, GB])
    xhat = sb("xhat1", [P, GB, D])
    xnF = sb("xnF1", [P, KD, GT])
    mask_i = sb("mask_i", [P, GT], I32)
    mask_f = sb("mask_f", [P, GT])
    k_e = sb("k_e", [P, KD, GT])
    kmax = sb("kmax", [P, KD, GB])
    ksum = sb("ksum", [P, KD, GB])
    v = sb("v", [P, GB, D])
    q = sb("q", [P, GB, D])
    qmax = sb("qmax", [P, GB, NH])
    qsum = sb("qsum", [P, GB, NH])
    kT = sb("kT", [P, GB, D])
    qF = sb("qF", [P, GB, KD, P])
    at = sb("at", [P, GB, KD, P])
    y = sb("y", [P, GB, D])
    yst = sb("yst", [P, GB, 6])
    ymv = sb("ymv", [P, GB, 2])
    yr = sb("yr", [P, 2, GB])
    yhat = sb("yhat", [P, GB, D])
    hp = sb("hp", [P, GB, D])
    ht = sb("ht", [P, GB, D])
    hF = sb("hF", [P, GB, D])
    xr = sb("xr", [P, GB, D])

    banks = [[ctx.enter_context(nc.psum_tensor(f"pair{i}{b}", [P, 512], F32)) for b in range(2)] for i in range(4)]

    names = ("w_in x_loaded mask_loaded xr_loaded out_stored "
             "bn_a st_a lnv_a rstd_a ln1_done xn_done mask_done k_emptied kmax_r kneg_done e_done rk_done es_done v_done "
             "q_emptied qmax_done qsub_done qe_done qsum_r rq_done kT_done qF_done at_done y_emptied bn_b st_b lnv_b rstd_b "
             "yhat_done hp_done h_step hsig_done hF_done xb_done f_done").split()
    s = {n: sem("p3_" + n) for n in names}
    f = {n: sem("p3_filled_" + n) for n in ("XN", "K", "V", "Q", "ET", "QT", "AT", "Y", "HT", "F")}

    def over_groups(eng, body):
        def peeled(g):
            body(g, g + 2 < NG, 0 <= g + 1 < NG, 0 <= g < NG, 0 <= g - 1)

        for g in range(-2, 2):
            peeled(g)
        with eng.Fori(0, NG - 4) as i:
            body(i + 2, True, True, True, True)
        for g in range(NG - 2, NG + 1):
            peeled(g)

    block = ctx.enter_context(nc.Block())

    @block.sync
    def _(sp):
        for w, name in ((wk, "Wk"), (wv, "Wv"), (wq, "Wq"), (wo, "Wo")):
            sp.dma_start(w[:, :, :], io[name].rearrange("(k p) n -> p k n", p=P)).then_inc(s["w_in"], 16)
        for t, name in ((bv, "bv"), (bq, "bq"), (bo, "bo")):
            sp.dma_start(t[:, :], io[name].partition_broadcast(P)).then_inc(s["w_in"], 16)
        for n, name in enumerate(("n_g", "n_b", "bk")):
            sp.dma_start(cols[:, n, :], io[name]).then_inc(s["w_in"], 16)
        sp.dma_start(heads[:, :], io["heads"]).then_inc(s["w_in"], 16)

        def body(g, S, A, B, Cc):
            sg, a, c = g + 2, g + 1, g - 1
            if S:
                sp_wait(sp, s["ln1_done"], sg * GB)
                sp.dma_start(x_in[:, :, :], io["x1"][bass.ds(sg * GB, GB), :, :].rearrange("b t d -> t b d")).then_inc(s["x_loaded"], 16)
            if A:
                sp_wait(sp, s["mask_done"], a)
                sp.dma_start(mask_i[:, :].rearrange("p (b t) -> p b t", b=GB),
                             io["mask"][bass.ds(a * GB, GB), :].partition_broadcast(P)).then_inc(s["mask_loaded"], 16)
            if Cc:
                sp_wait(sp, s["out_stored"], c * 16)
                sp.dma_start(xr[:, :, :], io["x1"][bass.ds(c * GB, GB), :, :].rearrange("b t d -> t b d")).then_inc(s["xr_loaded"], 16)
                sp_wait(sp, s["f_done"], c * GB + GB)
                sp.dma_start(io["out"][bass.ds(c * GB, GB), :, :].rearrange("b t d -> t b d"), xr[:, :, :]).then_inc(s["out_stored"], 16)

        over_groups(sp, body)
        sp.wait_ge(s["out_stored"], 16 * NG)

    @block.tensor
    def _(pe):
        ident = C["ident"][:, :]

        def turn(out, src):
            for k in range(KD):
                last = pe.transpose(out[:, k * P:(k + 1) * P], src[:, k * P:(k + 1) * P], ident)
            return last

        def product(out, lhs, w):
            for k in range(KD):
                last = pe.matmul(out[:, :], lhs(k), w[:, k, :], start=(k == 0), stop=(k == KD - 1))
            return last

        def body(g, S, A, B, Cc):
            a, c = g + 1, g - 1
            if B:
                for b in range(GB):
                    wait(pe, s["es_done"], g * 2 + 2)
                    wait(pe, s["f_done"], g * 2 + (b - 3))
                    for k in range(KD):
                        last = pe.transpose(banks[0][b][:, k * P:(k + 1) * P], k_e[:, k, b * P:(b + 1) * P], ident)
                    last.then_inc(f["ET"], 1)
            if A:
                for j in range(2):
                    wait(pe, s["ln1_done"], a * 2 + 2)
                    wait(pe, s["q_emptied"], a * 2 + (j - 1))
                    for e in range(2):
                        for b in range(GB):
                            o, k = (e * GB + b) * P, 2 * j + e
                            last = pe.transpose(banks[1][j][:, o:o + P], xhat[:, b, k * P:(k + 1) * P], ident)
                    last.then_inc(f["XN"], 1)
            if B:
                for b in range(GB):
                    wait(pe, s["qe_done"], g * 2 + (b + 1))
                    wait(pe, s["v_done"], g * 2 + (b + 1))
                    turn(banks[2][b], q[:, b, :]).then_inc(f["QT"], 1)
                for b in range(GB):
                    wait(pe, s["kT_done"], g * 2 + (b + 1))
                    wait(pe, s["v_done"], g * 2 + (b + 1))
                    wait(pe, s["y_emptied"], g * 2 + (b - 1))
                    for k in range(KD):
                        last = pe.matmul(banks[3][b][:, k * P:(k + 1) * P], v[:, b, k * P:(k + 1) * P],
                                         kT[:, b, k * P:(k + 1) * P], start=True, stop=True)
                    last.then_inc(f["AT"], 1)
            if Cc:
                for b in range(GB):
                    wait(pe, s["yhat_done"], c * 2 + (b + 1))
                    if B:
                        wait(pe, s["kT_done"], g * 2 + (b + 1))
                    wait(pe, s["f_done"], c * 2 + (b - 1))
                    turn(banks[0][b], yhat[:, b, :]).then_inc(f["HT"], 1)
            if A:
                if isinstance(g, int) and g == -1:
                    pe.wait_ge(s["w_in"], 16 * 11)
                for j in range(2):
                    wait(pe, s["xn_done"], a * 2 + 2)
                    for e in range(2):
                        for k in range(KD):
                            m = (2 * j + e) * P
                            last = pe.matmul(banks[1][j][:, e * GT:(e + 1) * GT], wk[:, k, m:m + P], xnF[:, k, :],
                                             start=(k == 0), stop=(k == KD - 1))
                    last.then_inc(f["K"], 1)

            def values(b):
                wait(pe, s["qF_done"], a * 2 + (b - 1))
                product(banks[2][b], lambda k: xnF[:, k, b * P:(b + 1) * P], wv).then_inc(f["V"], 1)

            def queries(b):
                wait(pe, s["k_emptied"], a * 2 + (b + 1))
                product(banks[1][b], lambda k: xnF[:, k, b * P:(b + 1) * P], wq).then_inc(f["Q"], 1)

            def film_product(b):
                wait(pe, s["hF_done"], c * 2 + (b + 1))
                product(banks[0][b], lambda k: hF[:, b, k * P:(k + 1) * P], wo).then_inc(f["F"], 1)

            if A:
                values(0)
            if B:
                for b in range(GB):
                    wait(pe, s["at_done"], g * 2 + (b + 1))
                    wait(pe, s["qF_done"], g * 2 + (b + 1))
                    for k in range(KD):
                        last = pe.matmul(banks[3][b][:, k * P:(k + 1) * P], qF[:, b, k, :], at[:, b, k, :], start=True, stop=True)
                    last.then_inc(f["Y"], 1)
            if A:
                values(1)
            if Cc:
                film_product(0)
            if A:
                queries(0)
            if Cc:
                film_product(1)
            if A:
                queries(1)

        over_groups(pe, body)

    @block.scalar
    def _(act):
        act.preload_act_table_set("natural_log_exp_and_others")

        def body(g, S, A, B, Cc):
            sg, a, c = g + 2, g + 1, g - 1
            if B:
                for b in range(GB):
                    wait(act, f["ET"], g * 2 + (b + 1))
                    act.activation(kT[:, b, :], banks[0][b][:, :], ACT.Copy).then_inc(s["kT_done"], 1)
            if A:
                if isinstance(g, int) and g == -1:
                    act.wait_ge(s["w_in"], 16 * 11)
                for j in range(2):
                    wait(act, f["XN"], a * 2 + (j + 1))
                    wait(act, f["Q"], a * 2)
                    for e in range(2):
                        k = 2 * j + e
                        last = act.activation(xnF[:, k, :], banks[1][j][:, e * GT:(e + 1) * GT], ACT.Identity,
                                              scale=cols[:, 0, k:k + 1], bias=cols[:, 1, k:k + 1])
                    last.then_inc(s["xn_done"], 1)
            if B:
                for b in range(GB):
                    wait(act, f["QT"], g * 2 + (b + 1))
                    act.activation(qF[:, b, :, :].rearrange("p k t -> p (k t)"), banks[2][b][:, :], ACT.Copy).then_inc(s["qF_done"], 1)
            if Cc:
                for b in range(GB):
                    wait(act, s["hp_done"], c * 2 + (b + 1))
                    wait(act, s["hF_done"], c * 2 + (b - 1))
                    act.activation(ht[:, b, :], hp[:, b, :], ACT.Exp, scale=-1.0).then_inc(s["h_step"], 1)
                for b in range(GB):
                    wait(act, s["h_step"], c * 4 + (b + 1))
                    act.activation(ht[:, b, :], ht[:, b, :], ACT.Ln, bias=1.0).then_inc(s["h_step"], 1)
                for b in range(GB):
                    wait(act, s["h_step"], c * 4 + (b + 3))
                    act.activation(ht[:, b, :], ht[:, b, :], ACT.Exp, scale=-1.0).then_inc(s["hsig_done"], 1)
            if A:
                for j in range(2):
                    wait(act, s["kneg_done"], a * 2 + (j + 1))
                    for e in range(2):
                        for b in range(GB):
                            k = 2 * j + e
                            blk = k_e[:, k, b * P:(b + 1) * P]
                            last = act.activation(blk, blk, ACT.Exp, bias=kmax[:, k, b:b + 1], accum_out=ksum[:, k, b:b + 1])
                    last.then_inc(s["e_done"], 1)
            if B:
                for b in range(GB):
                    wait(act, s["st_b"], g * 2 + (b + 1))
                    act.activation(yr[:, 0, b:b + 1], ymv[:, b, 1:2], ACT.Ln, bias=C["eps"][:, 0:1]).then_inc(s["lnv_b"], 1)
                for b in range(GB):
                    wait(act, s["lnv_b"], g * 2 + (b + 1))
                    act.activation(yr[:, 1, b:b + 1], yr[:, 0, b:b + 1], ACT.Exp, scale=-0.5).then_inc(s["rstd_b"], 1)
            if A:
                for b in range(GB):
                    wait(act, s["qsub_done"], a * 2 + (b + 1))
                    act.activation(q[:, b, :], q[:, b, :], ACT.Exp).then_inc(s["qe_done"], 1)
            if S:
                wait(act, s["st_a"], sg + 1)
                act.activation(rstd[:, 0, :], mv[:, :, 1], ACT.Ln, bias=C["eps"][:, 0:1]).then_inc(s["lnv_a"], 1)
                wait(act, s["lnv_a"], sg + 1)
                act.activation(rstd[:, 1, :], rstd[:, 0, :], ACT.Exp, scale=-0.5).then_inc(s["rstd_a"], 1)

        over_groups(act, body)

    @block.vector
    def _(dve):
        def by_head(t):
            return t.rearrange("p (h e) -> p h e", e=HD)

        dve.wait_ge(s["w_in"], 16 * 11)

        def body(g, S, A, B, Cc):
            sg, a, c = g + 2, g + 1, g - 1
            if A:
                wait(dve, s["mask_loaded"], a * 16 + 16)
                dve.tensor_scalar(mask_f[:, :], mask_i[:, :], 1.0, MASKED, ALU.is_equal, ALU.mult).then_inc(s["mask_done"], 1)
            if B:
                for b in range(GB):
                    wait(dve, f["AT"], g * 2 + (b + 1))
                    dve.tensor_tensor(at[:, b, :, :], banks[3][b][:, :].rearrange("p (k e) -> p k e", k=KD),
                                      heads[:, :].unsqueeze(1).broadcast_to([P, KD, P]), ALU.mult).then_inc(s["at_done"], 1)
            if Cc:
                for b in range(GB):
                    wait(dve, f["HT"], c * 2 + (b + 1))
                    wait(dve, s["hF_done"], c * 2 + (b - 1))
                    for k in range(KD):
                        last = dve.tensor_scalar(hp[:, b, k * P:(k + 1) * P], banks[0][b][:, k * P:(k + 1) * P],
                                                 C["gm1"][:, bass.ds(c * GB + b, 1), k], C["bm1"][:, bass.ds(c * GB + b, 1), k],
                                                 ALU.mult, ALU.add)
                    last.then_inc(s["hp_done"], 1)
            if A:
                wait(dve, s["mask_done"], a + 1)
                for j in range(2):
                    wait(dve, f["K"], a * 2 + (j + 1))
                    wait(dve, f["ET"], a * 2)
                    for e in range(2):
                        k = 2 * j + e
                        last = dve.scalar_tensor_tensor(k_e[:, k, :], banks[1][j][:, e * GT:(e + 1) * GT], cols[:, 2, k:k + 1],
                                                        mask_f[:, :], ALU.add, ALU.add)
                    last.then_inc(s["k_emptied"], 1)
                    wait(dve, s["k_emptied"], a * 2 + (j + 1))
                    km = kmax[:, 2 * j:2 * j + 2, :].rearrange("p k b -> p (k b)")
                    dve.tensor_reduce(km, k_e[:, 2 * j:2 * j + 2, :].rearrange("p k (b t) -> p (k b) t", b=GB), AX.X,
                                      ALU.max).then_inc(s["kmax_r"], 1)
                    wait(dve, s["kmax_r"], a * 2 + (j + 1))
                    dve.tensor_scalar(km, km, -1.0, None, ALU.mult).then_inc(s["kneg_done"], 1)

            def values(b):
                wait(dve, f["V"], a * 2 + (b + 1))
                dve.tensor_tensor(v[:, b, :], banks[2][b][:, :], bv[:, :], ALU.add).then_inc(s["v_done"], 1)

            if A:
                values(0)
            if B:
                for b in range(GB):
                    wait(dve, f["Y"], g * 2 + (b + 1))
                    wait(dve, s["rq_done"], g * 2 + (b + 1))
                    dve.tensor_tensor(by_head(y[:, b, :]), by_head(banks[3][b][:, :]),
                                      qsum[:, b, :].unsqueeze(2).broadcast_to([P, NH, HD]), ALU.mult).then_inc(s["y_emptied"], 1)
                    wait(dve, s["y_emptied"], g * 2 + (b + 1))
                    dve.bn_stats(yst[:, b, :], y[:, b, :]).then_inc(s["bn_b"], 1)
            if B:
                wait(dve, s["bn_b"], g * 2 + 2)
            if A:
                values(1)
            if B:
                for b in range(GB):
                    dve.bn_aggr(ymv[:, b, :], yst[:, b, :]).then_inc(s["st_b"], 1)
            if A:
                wait(dve, s["e_done"], a * 2 + 2)
                dve.reciprocal(ksum[:, :, :], ksum[:, :, :]).then_inc(s["rk_done"], 1)
            if B:
                wait(dve, f["HT"], g * 2)
                for b in range(GB):
                    wait(dve, s["rstd_b"], g * 2 + (b + 1))
                    dve.tensor_scalar(yhat[:, b, :], y[:, b, :], ymv[:, b, 0:1], yr[:, 1, b:b + 1], ALU.subtract,
                                      ALU.mult).then_inc(s["yhat_done"], 1)

            def result(b):
                wait(dve, f["F"], c * 2 + (b + 1))
                wait(dve, s["xb_done"], c * 2 + (b + 1))
                dve.tensor_tensor(xr[:, b, :], banks[0][b][:, :], xr[:, b, :], ALU.add).then_inc(s["f_done"], 1)

            def queries(b):
                wait(dve, f["Q"], a * 2 + (b + 1))
                dve.tensor_tensor(q[:, b, :], banks[1][b][:, :], bq[:, :], ALU.add).then_inc(s["q_emptied"], 1)
                wait(dve, s["q_emptied"], a * 2 + (b + 1))
                dve.tensor_reduce(qmax[:, b, :], by_head(q[:, b, :]), AX.X, ALU.max).then_inc(s["qmax_done"], 1)

            if Cc:
                result(0)
            if A:
                queries(0)
            if Cc:
                result(1)
            if A:
                queries(1)
            if S:
                wait(dve, s["x_loaded"], sg * 16 + 16)
                for b in range(GB):
                    dve.bn_stats(stats[:, b, :], x_in[:, b, :]).then_inc(s["bn_a"], 1)
                wait(dve, s["bn_a"], sg * 2 + 2)

            def sum_queries(b):
                wait(dve, s["qe_done"], a * 2 + (b + 1))
                dve.tensor_reduce(qsum[:, b, :], by_head(q[:, b, :]), AX.X, ALU.add).then_inc(s["qsum_r"], 1)

            if A:
                sum_queries(0)
            if S:
                for b in range(GB):
                    last = dve.bn_aggr(mv[:, b, :], stats[:, b, :])
                last.then_inc(s["st_a"], 1)
            if A:
                sum_queries(1)
                for b in range(GB):
                    wait(dve, s["qsum_r"], a * 2 + (b + 1))
                    dve.reciprocal(qsum[:, b, :], qsum[:, b, :]).then_inc(s["rq_done"], 1)
            if S:
                wait(dve, f["XN"], sg * 2)
                wait(dve, s["rstd_a"], sg + 1)
                for b in range(GB):
                    dve.tensor_scalar(xhat[:, b, :], x_in[:, b, :], mv[:, b, 0:1], rstd[:, 1, b:b + 1], ALU.subtract,
                                      ALU.mult).then_inc(s["ln1_done"], 1)

        over_groups(dve, body)

    @block.gpsimd
    def _(gps):
        gps.wait_ge(s["w_in"], 16 * 11)

        def body(g, S, A, B, Cc):
            a, c = g + 1, g - 1
            if Cc:
                wait(gps, s["xr_loaded"], c * 16 + 16)
                for b in range(GB):
                    gps.tensor_tensor(xr[:, b, :], xr[:, b, :], bo[:, :], ALU.add).then_inc(s["xb_done"], 1)
                for b in range(GB):
                    wait(gps, s["hsig_done"], c * 2 + (b + 1))
                    wait(gps, f["F"], c * 2 + (b - 1))
                    gps.tensor_tensor(hF[:, b, :], hp[:, b, :], ht[:, b, :], ALU.mult).then_inc(s["hF_done"], 1)
            if A:
                for j in range(2):
                    wait(gps, s["rk_done"], a + 1)
                    blk = k_e[:, 2 * j:2 * j + 2, :].rearrange("p k (b t) -> p (k b) t", b=GB)
                    r = ksum[:, 2 * j:2 * j + 2, :].rearrange("p k b -> p (k b)").unsqueeze(2).broadcast_to([P, 4, P])
                    gps.tensor_tensor(blk, blk, r, ALU.mult).then_inc(s["es_done"], 1)
                for b in range(GB):
                    wait(gps, s["qmax_done"], a * 2 + (b + 1))
                    blk = q[:, b, :].rearrange("p (h e) -> p h e", e=HD)
                    gps.tensor_tensor(blk, blk, qmax[:, b, :].unsqueeze(2).broadcast_to([P, NH, HD]), ALU.subtract).then_inc(s["qsub_done"], 1)

        over_groups(gps, body)


def setup(nc, ctx, NB, W, C, io):

    def sb(name, shape, dt=F32):
        return ctx.enter_context(nc.sbuf_tensor(name, shape, dt))

    def sem(name):
        return ctx.enter_context(nc.semaphore(name))

    KC = COND // P
    cT = sb("cT", [P, KC, NB])
    ec = sb("ec", [P, KC, NB])
    ada = sb("ada", [P, KC, 3 * D])
    film = sb("film", [P, KC, 2 * D])
    cols = sb("cols", [P, 9, KD])
    one_plus = sb("one_plus", [P, 2, KD])
    t0 = sb("t0", [P, 2, KD, NB])
    gbias = sb("gbias", [NB, D])
    gate = sb("gate", [NB, D])
    ps = [ctx.enter_context(nc.psum_tensor(f"mod{i}", [P, 512], F32)) for i in range(5)]

    cond_in, mats_in, cols_in, gbias_in, weights_in, gate_out = (
        sem(n) for n in ("cond_in", "mats_in", "cols_in", "gbias_in", "weights_in", "gate_out"))
    silu_e, silu_v, mod_done, mod_v, gate_v, a_exp = (sem(n) for n in ("silu_e", "silu_v", "mod_done", "mod_v", "gate_v", "a_exp"))
    LN_G, LN_B, SHIFT, SCALE, F_SCALE, F_SHIFT, F_G, F_B = range(8)

    block = ctx.enter_context(nc.Block())

    @block.sync
    def _(sp):
        sp.dma_start(cT[:, :, :], io["condT"].rearrange("(k p) b -> p k b", p=P)).then_inc(cond_in, 16)
        ada_v = io["adaT"].rearrange("(k p) n -> p k n", p=P)
        film_v = io["filmW"].rearrange("(k p) n -> p k n", p=P)
        for k in range(KC):
            sp.dma_start(ada[:, k, :], ada_v[:, k, :]).then_inc(mats_in, 16)
        for k in range(KC):
            sp.dma_start(film[:, k, :], film_v[:, k, :]).then_inc(mats_in, 16)
        for i, name in enumerate(("ln_g", "ln_b", "b_shift", "b_scale", "bf_scale", "bf_shift", "fn_g", "fn_b")):
            sp.dma_start(cols[:, i, :], io[name]).then_inc(cols_in, 16)
        sp.dma_start(gbias[:, :], io["b_gate"].partition_broadcast(NB)).then_inc(gbias_in, 16)
        sp.dma_start(C["ident"][:, :], io["ident"]).then_inc(weights_in, 16)
        sp.dma_start(C["cw"][:, :, :], io["conv_w"]).then_inc(weights_in, 16)
        sp.dma_start(C["cb"][:, :], io["conv_b"]).then_inc(weights_in, 16)
        sp.dma_start(C["A"][:, :, :], io["A_log"].rearrange("(k p) n -> p k n", p=P)).then_inc(weights_in, 16)
        sp.dma_start(C["dbc"][:, :], io["D"].partition_broadcast(P)).then_inc(weights_in, 16)
        sp.dma_start(W["dt"][0:RANK, :], io["dtT"]).then_inc(weights_in, 16)
        sp.dma_start(W["dt"][RANK:RANK + 1, :], io["dt_b"]).then_inc(weights_in, 16)
        sp.dma_start(W["x"][:, :, :], io["xT"].rearrange("(k p) n -> p k n", p=P)).then_inc(weights_in, 16)
        for k in range(KD):
            sp.dma_start(W["in"][:, k, :], io["inT"].rearrange("(k p) n -> p k n", p=P)[:, k, :]).then_inc(weights_in, 16)
        sp.dma_start(W["out"][:, :, :], io["outT"].rearrange("(k p) n -> p k n", p=P)).then_inc(weights_in, 16)
        sp.wait_ge(weights_in, 16 * (9 + KD))
        sp.wait_ge(gate_v, 1)
        sp.dma_start(io["gate"], gate[:, :]).then_inc(gate_out, 16)
        sp.wait_ge(gate_out, 16)

    @block.scalar
    def _(act):
        act.preload_act_table_set("natural_log_exp_and_others")
        act.wait_ge(cond_in, 16)
        act.activation(ec[:, :, :], cT[:, :, :], ACT.Exp, scale=-1.0).then_inc(silu_e, 1)
        act.wait_ge(weights_in, 16 * (9 + KD))
        act.activation(C["A"][:, :, :], C["A"][:, :, :], ACT.Exp).then_inc(a_exp, 1)

    @block.tensor
    def _(pe):
        pe.wait_ge(silu_v, 3)
        pe.wait_ge(mats_in, 16 * 2 * KC)
        for i, (m, off) in enumerate(((ada, 0), (ada, D), (film, 0), (film, D))):
            for k in range(KD):
                for c in range(KC):
                    last = pe.matmul(ps[i][:, k * NB:(k + 1) * NB], m[:, c, off + k * P:off + (k + 1) * P], cT[:, c, :],
                                     start=(c == 0), stop=(c == KC - 1))
        for c in range(KC):
            last = pe.matmul(ps[4][0:NB, :], cT[:, c, :], ada[:, c, 2 * D:3 * D], start=(c == 0), stop=(c == KC - 1))
        last.then_inc(mod_done, 1)

    @block.vector
    def _(dve):
        dve.wait_ge(silu_e, 1)
        dve.tensor_scalar(ec[:, :, :], ec[:, :, :], 1.0, None, ALU.add).then_inc(silu_v, 1)
        dve.wait_ge(silu_v, 1)
        dve.reciprocal(ec[:, :, :], ec[:, :, :]).then_inc(silu_v, 1)
        dve.wait_ge(silu_v, 2)
        dve.tensor_tensor(cT[:, :, :], cT[:, :, :], ec[:, :, :], ALU.mult).then_inc(silu_v, 1)
        dve.wait_ge(cols_in, 16 * 8)
        dve.tensor_scalar(one_plus[:, 0, :], cols[:, SCALE, :], 1.0, None, ALU.add).then_inc(mod_v, 1)
        dve.tensor_scalar(one_plus[:, 1, :], cols[:, F_SCALE, :], 1.0, None, ALU.add).then_inc(mod_v, 1)
        dve.wait_ge(mod_v, 2)
        dve.wait_ge(mod_done, 1)
        for i, (scale, shift, g, b, gm, bm) in enumerate(((1, 0, LN_G, LN_B, "gm0", "bm0"), (2, 3, F_G, F_B, "gm1", "bm1"))):
            for k in range(KD):
                sc = ps[scale][:, k * NB:(k + 1) * NB]
                dve.tensor_scalar(C[gm][:, :, k], sc, one_plus[:, i, k:k + 1], cols[:, g, k:k + 1], ALU.add, ALU.mult)
                dve.tensor_scalar(t0[:, i, k, :], sc, one_plus[:, i, k:k + 1], cols[:, b, k:k + 1], ALU.add,
                                  ALU.mult).then_inc(mod_v, 1)
        dve.wait_ge(mod_v, 2 + 2 * KD)
        for i, (shift, bias, bm) in enumerate(((0, SHIFT, "bm0"), (3, F_SHIFT, "bm1"))):
            for k in range(KD):
                dve.scalar_tensor_tensor(C[bm][:, :, k], ps[shift][:, k * NB:(k + 1) * NB], cols[:, bias, k:k + 1],
                                         t0[:, i, k, :], ALU.add, ALU.add)
        dve.wait_ge(gbias_in, 16)
        dve.tensor_tensor(gate[:, :], ps[4][0:NB, :], gbias[:, :], ALU.add).then_inc(gate_v, 1)
        dve.wait_ge(weights_in, 16 * (9 + KD))
        for e in range(KI):
            for t in range(TAPS):
                dve.tensor_scalar(W["conv"][:, e, t, :], C["ident"][:, :], C["cw"][:, e, t:t + 1], None, ALU.mult)
        dve.tensor_scalar(C["ncb"][:, :], C["cb"][:, :], -1.0, None, ALU.mult)
        dve.memset(C["eps"][:, :], EPS)
        dve.wait_ge(a_exp, 1)
        dve.tensor_scalar(C["A"][:, :, :], C["A"][:, :, :], -1.0, None, ALU.mult)


def program(nc, io, NB):
    NG = NB // GB
    with ExitStack() as all_parts:
        def const(stack, where, name, shape):
            where[name] = stack.enter_context(nc.sbuf_tensor("c_" + name, shape, F32))

        C, W = {}, {}
        for name, shape in (("ident", [P, P]), ("gm0", [P, NB, KD]), ("bm0", [P, NB, KD]), ("gm1", [P, NB, KD]), ("bm1", [P, NB, KD]),
                            ("eps", [P, 1])):
            const(all_parts, C, name, shape)
        with ExitStack() as layer0:
            for name, shape in (("A", [P, KI, NST]), ("cw", [P, KI, TAPS]), ("cb", [P, KI]), ("ncb", [P, KI]), ("dbc", [P, DI])):
                const(layer0, C, name, shape)
            for name, shape in (("in", [P, KD, 2 * DI]), ("x", [P, KI, RANK + 2 * NST]), ("dt", [RANK + 1, DI]),
                                ("out", [P, KI, D]), ("conv", [P, KI, TAPS, P])):
                const(layer0, W, name + "_w", shape)
                W[name] = W[name + "_w"]
            with ExitStack() as ctx:
                setup(nc, ctx, NB, W, C, io)
            with ExitStack() as ctx:
                mamba(nc, ctx, NG, W, C, io)
        with ExitStack() as ctx:
            attention(nc, ctx, NG, C, io)


def arrays_of(inputs):
    import numpy as np

    def T(a):
        return np.ascontiguousarray(np.asarray(a).T)

    def col(v):
        v = np.asarray(v)
        return np.ascontiguousarray(v.reshape(-1, P).T)

    i = {k: np.asarray(v) for k, v in inputs.items()}
    L0, L1 = "L0_cond_", "L1_cond_"
    ada_b, film_b = i[L0 + "ada_b"], i[L1 + "film_emb_b"]
    heads = np.kron(np.eye(P // HD, dtype=np.float32), np.ones((HD, HD), np.float32))
    return {
        "x": i["x"], "condT": T(i["cond_2048"]), "mask": i["mask_BxS_ik0"],
        "adaT": T(i[L0 + "ada_w"]), "filmW": i[L1 + "film_emb_W"],
        "ln_g": col(i[L0 + "ln_g"]), "ln_b": col(i[L0 + "ln_b"]),
        "b_shift": col(ada_b[:D]), "b_scale": col(ada_b[D:2 * D]), "b_gate": ada_b[2 * D:].copy(),
        "bf_scale": col(film_b[:D]), "bf_shift": col(film_b[D:]),
        "fn_g": col(i[L1 + "film_norm_scale"]), "fn_b": col(i[L1 + "film_norm_bias"]),
        "ident": np.eye(P, dtype=np.float32), "heads": heads,
        "conv_w": np.ascontiguousarray(i[L0 + "conv_w"].reshape(KI, P, TAPS).transpose(1, 0, 2)), "conv_b": col(i[L0 + "conv_b"]),
        "A_log": i[L0 + "A_log"], "D": i[L0 + "D_param"],
        "dtT": T(i[L0 + "dt_proj_w"]), "dt_b": i[L0 + "dt_proj_b"].reshape(1, DI), "xT": T(i[L0 + "x_proj_w"]),
        "inT": T(i[L0 + "in_proj_w"]), "outT": T(i[L0 + "out_proj_w"]),
        "n_g": col(i[L1 + "norm_scale"]), "n_b": col(i[L1 + "norm_bias"]),
        "Wq": i[L1 + "Wq"], "Wk": i[L1 + "Wk"], "Wv": i[L1 + "Wv"], "Wo": i[L1 + "film_out_W"],
        "bq": i[L1 + "bq"], "bk": col(i[L1 + "bk"]), "bv": i[L1 + "bv"], "bo": i[L1 + "film_out_b"],
    }


def kernel(**inputs):
    import numpy as _np
    import concourse.bacc as _bacc
    from concourse import mybir as _mybir
    from concourse.bass_utils import run_bass_kernel_spmd as _run

    nc = _bacc.Bacc("TRN2", target_bir_lowering=False, num_devices=1)
    arrays = {f"in_{k}": _np.ascontiguousarray(v) for k, v in arrays_of(inputs).items()}
    NB = arrays["in_x"].shape[0]
    io = {k[3:]: nc.dram_tensor(k, v.shape, _mybir.dt.from_np(v.dtype), kind="ExternalInput").ap() for k, v in arrays.items()}
    io["gate"] = nc.dram_tensor("gate_scratch", (NB, D), F32, kind="Internal").ap()
    io["b"] = nc.dram_tensor("b_scratch", (NST, GT), F32, kind="Internal").ap()
    io["x1"] = nc.dram_tensor("x1_scratch", (NB, P, D), F32, kind="Internal").ap()
    io["out"] = nc.dram_tensor("out_0", (NB, P, D), F32, kind="ExternalOutput").ap()
    program(nc, io, NB)
    r = _run(nc, [arrays], core_ids=[0])
    return r.results[0]["out_0"]
```

```python
from contextlib import ExitStack

import concourse.bass as bass
from concourse import mybir

F32 = mybir.dt.float32
I32 = mybir.dt.int32
ALU = mybir.AluOpType
ACT = mybir.ActivationFunctionType
AX = mybir.AxisListType

P = 128
D = 512
DI = 1024
NST = 16
RANK = 64
TAPS = 4
COND = 1024
HD = 32
EPS = 1e-5
KD = D // P
KI = DI // P
GB = 2
GT = GB * P
QUARTERS = NST * 4


def wait(eng, sem, value):
    if isinstance(value, int) and value <= 0:
        return
    eng.wait_ge(sem, value)


def sp_wait(sp, sem, value):
    wait(sp, sem, value)
    sp.nop(nofuse=True)


SIDE = [
    ("Z", 0, [0, 0, 1, 3]),
    ("Z", 1, [3, 3, 4, 5]),
    ("Z", 2, [6, 7, 7, 8]),
    ("Z", 3, [8, 8, 10, 11]),
    ("XN", 0, [13]),
    ("XN", 1, [13]),
    ("YT", 0, [15]),
    ("XI", 0, [15, 15, 16, 17]),
    ("XI", 1, [18, 19, 21, 21]),
    ("CV", 0, [23, 23, 23, 23]),
    ("XI", 2, [24, 25, 25, 25]),
    ("YT", 1, [25]),
    ("YT", 2, [26]),
    ("CV", 1, [26, 27, 27, 28]),
    ("CV", 2, [30, 30, 30, 31]),
    ("XI", 3, [31, 31, 31, 33]),
    ("YT", 3, [33]),
    ("CV", 3, [34, 34, 34, 37]),
    ("O", 0, [37, 37, 37, 37, 37, 38, 40, 40]),
    ("O", 1, [43, 43, 44, 45, 45, 46, 47, 47]),
    ("UT", 0, [48]),
    ("XP", 0, [49, 51, 51, 51]),
    ("BC", 0, [51]),
    ("UT", 1, [51]),
    ("UT", 2, [51]),
    ("UT", 3, [53]),
    ("DT", 0, [54]),
    ("DT", 1, [55]),
    ("DT", 2, [57]),
    ("DT", 3, [58]),
]
POST = ("Z", "YT", "O")
N_POST = sum(kind in POST for kind, _, _ in SIDE)
N_PRE = len(SIDE) - N_POST
SIGS = ("Z", "CV", "DT")
UT_BLOCK = [(0, 0), (1, 0), (0, 1), (1, 1)]
Z_BLOCK = [(0, 0), (0, 1), (1, 0), (1, 1)]

PARTS = {"Z": 4, "O": 8, "XI": 4, "CV": 4, "XP": 4, "DT": 1, "XN": 1, "YT": 1, "UT": 1, "BC": 1}
A_AFTER = {"Z": 2, "CV": 2, "DT": 3, "XN": 3, "XI": 3, "XP": 3, "YT": 3}
D_AFTER = {"Z": 3, "CV": 3, "DT": 4, "O": 3, "BC": 3, "UT": 3}
G_AFTER = {"Z": 5, "O": 6}
T_LAG = 2
C_LAG = 5
H_RING = 8
B_RING = 4
Q_STATS, Q_RSTD, Q_XHAT = 1, 4, 5


def side_of(post, pre):
    some = [e for e in SIDE if (post if e[0] in POST else pre)]
    return [(*e, c) for c, e in enumerate(some)]


def mamba(nc, ctx, NG, W, C, io):

    def sb(name, shape, dt=F32):
        return ctx.enter_context(nc.sbuf_tensor(name, shape, dt))

    def sem(name):
        return ctx.enter_context(nc.semaphore(name))

    x_in = sb("x_in", [P, GB, D])
    xhat = sb("xhat", [P, GB, D])
    stats = sb("stats", [P, GB, 6])
    mv = sb("mv", [P, GB, 2])
    lnv = sb("lnv", [P, GB])
    rstd = sb("rstd", [P, GB])
    xnF = [sb(f"xnF{i}", [P, KD, GT]) for i in range(2)]
    xin = sb("xin", [P, KI, GB, TAPS - 1 + P])
    u = [sb(f"u{i}", [P, KI, GT]) for i in range(2)]
    tmp = [sb(f"tmp{i}", [P, D]) for i in range(2)]
    dtr = sb("dtr", [RANK + 1, GT])
    dt = [sb(f"dt{i}", [P, KI, GT]) for i in range(2)]
    yzF = [a[:, :, :].rearrange("p k (b t) -> p k b t", b=GB) for a in dt]
    brow = sb("brow", [RANK + NST, GT])
    bbc = sb("bbc", [P, NST, GT])
    acc = [sb(f"acc{i}", [P, GB, DI]) for i in range(2)]
    ct = [sb(f"ct{i}", [P, GB, NST]) for i in range(2)]
    dbu = [sb(f"dbu{i}", [P, 2, GT]) for i in range(B_RING)]
    h = [sb(f"h{i}", [P, D]) for i in range(H_RING)]
    gb = sb("gb", [P, GB, D])
    xres = sb("xres", [P, GB, D])

    bank = [ctx.enter_context(nc.psum_tensor(f"side{i}", [P, 512], F32)) for i in range(2)]
    dA = [ctx.enter_context(nc.psum_tensor(f"dA{i}", [P, 2, GB, P], F32)) for i in range(2)]
    hT = [[ctx.enter_context(nc.psum_tensor(f"hT{i}{b}", [P, 512], F32)) for b in range(GB)] for i in range(2)]

    x_loaded, xres_loaded, gate_loaded, x1_stored = (sem(n) for n in ("x_loaded", "xres_loaded", "gate_loaded", "x1_stored"))
    init_done, dA_ready, dbu_ready, scan_done, ht_filled, c_dve, b_stored = (
        sem(n) for n in ("init_done", "dA_ready", "dbu_ready", "scan_done", "ht_filled", "c_dve", "b_stored"))
    b_loaded = [sem(f"b_loaded{k}") for k in range(4)]
    bn_done, stats_done, lnv_done, rstd_done, xhat_done, filled, act_step, sig_ready = (
        sem(n) for n in ("bn_done", "stats_done", "lnv_done", "rstd_done", "xhat_done", "filled", "act_step", "sig_ready"))
    xn_done, xin_done, u_done, brow_done, dtr_done, bc_done, dt_done, acc_init, du_done = (
        sem(n) for n in ("xn_done", "xin_done", "u_done", "brow_done", "dtr_done", "bc_done", "dt_done", "acc_init", "du_done"))
    zs_done, yz_done, yzf_done, og_done, x1_done = (sem(n) for n in ("zs_done", "yz_done", "yzf_done", "og_done", "x1_done"))

    def before(g, n_pre, n_post):
        if isinstance(g, int):
            return n_pre * min(g + 1, NG) + n_post * max(g - 1, 0)
        return g * (n_pre + n_post) + (n_pre - n_post)

    def emptied(kind, j, gp, gq):
        s, n, g = {
            "Z": (zs_done, 4, gq), "YT": (yzf_done, 4, gq), "O": (og_done, 2, gq), "XN": (xn_done, 2, gp),
            "XI": (xin_done, 4, gp), "CV": (u_done, 4, gp), "XP": (dtr_done, 1, gp), "BC": (bc_done, 1, gp),
            "DT": (dt_done, 4, gp), "UT": (acc_init, 4, gp)}[kind]
        return s, g * n + (j + 1)

    def over_groups(eng, body):
        body(-1, 1, False, False, True)
        body(0, 0, True, False, True)
        with eng.Fori(0, (NG - 2) // 2) as i:
            body(i * 2 + 1, 1, True, True, True)
            body(i * 2 + 2, 0, True, True, True)
        body(NG - 1, (NG - 1) % 2, True, True, False)
        body(NG, NG % 2, False, True, False)

    def sum_at(g, q, scan, post):
        v = q - C_LAG
        if v >= 0:
            return (g, v // 2, v % 2) if scan else None
        return (g - 1, (QUARTERS + v) // 2, v % 2) if post else None

    def temporary_free(eng, sig, sigs, g, gp, gq):
        if sig >= 2:
            kind, j = sigs[sig - 2]
            s, n, of = {"Z": (yz_done, 4, gq), "CV": (u_done, 4, gp), "DT": (dt_done, 4, gp)}[kind]
            wait(eng, s, of * n + (j + 1))
        elif isinstance(g, int) and g == NG:
            wait(eng, yz_done, (gq - 1) * 4 + (3 + sig))
        else:
            wait(eng, dt_done, g * 4 + (3 + sig))

    block = ctx.enter_context(nc.Block())

    @block.sync
    def _(sp):
        def body(g, par, scan, post, pre):
            gp, gq = g + 1, g - 1
            if pre:
                sp_wait(sp, xhat_done, gp * GB)
                sp.dma_start(x_in[:, :, :], io["x"][bass.ds(gp * GB, GB), :, :].rearrange("b t d -> t b d")).then_inc(x_loaded, 16)
            if scan:
                sp_wait(sp, dbu_ready, g * QUARTERS)
                sp.dma_start(bbc[:, 12:16, :], io["b"][12:16, :].partition_broadcast(P)).then_inc(b_loaded[3], 16)
            if post:
                sp.dma_start(xres[:, :, :], io["x"][bass.ds(gq * GB, GB), :, :].rearrange("b t d -> t b d")).then_inc(xres_loaded, 16)
                sp.dma_start(gb[:, :, :], io["gate"][bass.ds(gq * GB, GB), :].partition_broadcast(P)).then_inc(gate_loaded, 16)
                sp_wait(sp, x1_done, gq * GB + GB)
                sp.dma_start(io["x1"][bass.ds(gq * GB, GB), :, :].rearrange("b t d -> t b d"), xres[:, :, :]).then_inc(x1_stored, 16)
            if pre:
                sp_wait(sp, b_loaded[3], 16 * gp)
                sp_wait(sp, brow_done, gp + 1)
                sp.dma_start(io["b"], brow[RANK:RANK + NST, :]).then_inc(b_stored, 16)
                sp_wait(sp, b_stored, 16 * gp + 16)
                for k in range(3):
                    if scan:
                        sp_wait(sp, dbu_ready, g * QUARTERS + 16 * (k + 1))
                    sp.dma_start(bbc[:, 4 * k:4 * k + 4, :], io["b"][4 * k:4 * k + 4, :].partition_broadcast(P)).then_inc(b_loaded[k], 16)
            if post:
                sp_wait(sp, x1_stored, gq * 16 + 16)

        over_groups(sp, body)
        sp.wait_ge(x1_stored, 16 * NG)

    @block.tensor
    def _(pe):
        def fill_ht(g, q):
            half, n = (q // 2) % 2, q // 4
            wait(pe, scan_done, g * QUARTERS + (q + 1))
            if q % 2 == 0:
                wait(pe, c_dve, g * QUARTERS + (4 * n if half else 4 * n - 2))
            for e in range(2):
                for b in range(GB):
                    dst = ((q % 2) * 2 + e) * P
                    last = pe.transpose(hT[half][b][:, dst:dst + P],
                                        h[q % H_RING][:, (e * GB + b) * P:(e * GB + b + 1) * P], C["ident"][:, :])
            last.then_inc(ht_filled, 1)

        def piece(kind, j, c, part, gp, gq, par):
            nxt = 1 - par
            out = bank[c % 2]
            half, two = part // 2, (2 * (part % 2), 2 * (part % 2) + 1)
            if kind == "Z":
                b, hf = Z_BLOCK[j]
                last = pe.matmul(out[:, :], xnF[nxt][:, part, b * P:(b + 1) * P],
                                 W["in"][:, part, DI + hf * D:DI + (hf + 1) * D], start=(part == 0), stop=(part == KD - 1))
            elif kind == "YT":
                b, hf = Z_BLOCK[j]
                wait(pe, yz_done, gq * 4 + (j + 1))
                for k in range(4):
                    s = hf * D + k * P
                    last = pe.transpose(out[:, k * P:(k + 1) * P], acc[nxt][:, b, s:s + P], C["ident"][:, :])
            elif kind == "O":
                if part == 0:
                    wait(pe, yzf_done, gq * 4 + 2 * (j + 1))
                last = pe.matmul(out[:, :], yzF[nxt][:, part, j, :], W["out"][:, part, :], start=(part == 0), stop=(part == KI - 1))
            elif kind == "XN":
                wait(pe, xhat_done, gp * GB + GB)
                for e in range(2):
                    for b in range(GB):
                        s, k = (e * GB + b) * P, 2 * j + e
                        last = pe.transpose(out[:, s:s + P], xhat[:, b, k * P:(k + 1) * P], C["ident"][:, :])
            elif kind == "XI":
                if part == 0:
                    wait(pe, xn_done, gp * 2 + 2)
                e = 2 * j + half
                for k in two:
                    last = pe.matmul(out[:, half * GT:(half + 1) * GT], W["in"][:, k, e * P:(e + 1) * P],
                                     xnF[nxt][:, k, :], start=(k == 0), stop=(k == KD - 1))
            elif kind == "CV":
                if part == 0:
                    wait(pe, xin_done, gp * 4 + (j + 1))
                e = 2 * j + half
                for t in two:
                    last = pe.matmul(out[:, half * GT:(half + 1) * GT].rearrange("p (b t) -> p b t", b=GB),
                                     W["conv"][:, e, t, :], xin[:, e, :, t:t + P], start=(t == 0), stop=(t == TAPS - 1))
            elif kind == "XP":
                if part == 0:
                    wait(pe, u_done, gp * 4 + 4)
                for k in (2 * part, 2 * part + 1):
                    last = pe.matmul(out[0:RANK + NST, 0:GT], W["x"][:, k, 0:RANK + NST], u[nxt][:, k, :],
                                     start=(k == 0), stop=(k == KI - 1))
            elif kind == "BC":
                wait(pe, u_done, gp * 4 + 4)
                for b in range(GB):
                    for k in range(KI):
                        last = pe.matmul(out[:, b * NST:(b + 1) * NST], u[nxt][:, k, b * P:(b + 1) * P],
                                         W["x"][:, k, RANK + NST:RANK + 2 * NST], start=(k == 0), stop=(k == KI - 1))
            elif kind == "DT":
                wait(pe, dtr_done, gp + 1)
                for i in range(2):
                    e = 2 * j + i
                    last = pe.matmul(out[:, i * GT:(i + 1) * GT], W["dt"][:, e * P:(e + 1) * P], dtr[:, :], start=True, stop=True)
            elif kind == "UT":
                b, hf = UT_BLOCK[j]
                wait(pe, u_done, gp * 4 + 2 * (hf + 1))
                for k in range(4):
                    last = pe.transpose(out[:, k * P:(k + 1) * P], u[nxt][:, hf * 4 + k, b * P:(b + 1) * P], C["ident"][:, :])
            if part == PARTS[kind] - 1:
                last.then_inc(filled, 1)

        def bank_free(c, side, g, gp, gq):
            if c >= 2:
                wait(pe, *emptied(side[c - 2][0], side[c - 2][1], gp, gq))
            else:
                last_side = side_of(False, True) if not (isinstance(g, int) and g == NG) else side_of(True, False)
                wait(pe, *emptied(last_side[c - 2][0], last_side[c - 2][1], g, gq - 1))

        def body(g, par, scan, post, pre):
            gp, gq = g + 1, g - 1
            side = side_of(post, pre)
            for q in range(QUARTERS):
                if q >= T_LAG and scan:
                    fill_ht(g, q - T_LAG)
                if q < T_LAG and post:
                    fill_ht(g - 1, QUARTERS - T_LAG + q)
                for kind, j, at, c in side:
                    for part in range(PARTS[kind]):
                        if q == at[part]:
                            if part == 0:
                                bank_free(c, side, g, gp, gq)
                            piece(kind, j, c, part, gp, gq, par)

        pe.wait_ge(init_done, 4)
        over_groups(pe, body)

    @block.scalar
    def _(act):
        act.preload_act_table_set("natural_log_exp_and_others")
        act.wait_ge(init_done, 4)

        def decay(g, q, e, par):
            k, n = 2 * (q % 4) + e, q // 4
            last = act.activation(dA[q % 2][:, e, :, 1:P], dt[par][:, k, :].rearrange("p (b t) -> p b t", b=GB)[:, :, 1:P],
                                  ACT.Exp, scale=C["A"][:, k, n:n + 1])
            if e == 1:
                last.then_inc(dA_ready, 1)

        def simple(kind, j, c, g, gp, gq, par):
            nxt = 1 - par
            src = bank[c % 2]
            wait(act, filled, before(g, N_PRE, N_POST) + (c + 1))
            if kind == "XN":
                for part in range(2):
                    for b in range(GB):
                        k, s = 2 * j + part, (part * GB + b) * P
                        last = act.activation(xnF[nxt][:, k, b * P:(b + 1) * P], src[:, s:s + P], ACT.Identity,
                                              scale=C["gm0"][:, bass.ds(gp * GB + b, 1), k], bias=C["bm0"][:, bass.ds(gp * GB + b, 1), k])
                last.then_inc(xn_done, 1)
            elif kind == "XI":
                act.activation(xin[:, 2 * j:2 * j + 2, :, TAPS - 1:].rearrange("p e b t -> p (e b) t"),
                               src[:, :].rearrange("p (e b t) -> p (e b) t", e=2, b=GB), ACT.Copy).then_inc(xin_done, 1)
            elif kind == "XP":
                wait(act, b_stored, 16 * gp)
                act.activation(brow[RANK:RANK + NST, :], src[RANK:RANK + NST, 0:GT], ACT.Copy).then_inc(brow_done, 1)
                act.activation(dtr[0:RANK, :], src[0:RANK, 0:GT], ACT.Copy).then_inc(dtr_done, 1)
            elif kind == "YT":
                b, hf = Z_BLOCK[j]
                act.activation(yzF[nxt][:, 4 * hf:4 * hf + 4, b, :], src[:, :].rearrange("p (k t) -> p k t", k=4),
                               ACT.Copy).then_inc(yzf_done, 1)

        def staged(kind, j, c, stage, sig, sigs, g, gp, gq):
            src, t = bank[c % 2], tmp[sig % 2]
            step = before(g, 16, 8) + 2 * sig
            if stage == 0:
                wait(act, filled, before(g, N_PRE, N_POST) + (c + 1))
                temporary_free(act, sig, sigs, g, gp, gq)
                if kind == "Z":
                    act.activation(t[:, :], src[:, :], ACT.Exp, scale=-1.0).then_inc(act_step, 1)
                elif kind == "CV":
                    for e in range(2):
                        last = act.activation(t[:, e * GT:(e + 1) * GT], src[:, e * GT:(e + 1) * GT], ACT.Exp, scale=-1.0,
                                              bias=C["ncb"][:, 2 * j + e:2 * j + e + 1])
                    last.then_inc(act_step, 1)
                else:
                    act.activation(t[:, :], src[:, :], ACT.Abs).then_inc(act_step, 1)
            elif stage == 1:
                wait(act, act_step, step + 1)
                if kind == "DT":
                    act.activation(t[:, :], t[:, :], ACT.Exp, scale=-1.0).then_inc(act_step, 1)
                else:
                    act.activation(t[:, :], t[:, :], ACT.Ln, bias=1.0).then_inc(act_step, 1)
            else:
                wait(act, act_step, step + 2)
                if kind == "DT":
                    act.activation(t[:, :], t[:, :], ACT.Ln, bias=1.0).then_inc(sig_ready, 1)
                else:
                    act.activation(t[:, :], t[:, :], ACT.Exp, scale=-1.0).then_inc(sig_ready, 1)

        def body(g, par, scan, post, pre):
            gp, gq = g + 1, g - 1
            side = side_of(post, pre)
            sig_of = {c: i for i, c in enumerate(c for kind, _, _, c in side if kind in SIGS)}

            sigs = [(kind, j) for kind, j, _, _ in side if kind in SIGS]

            def stages(q, stage, later):
                for kind, j, at, c in side:
                    if kind in SIGS and q == at[-1] + A_AFTER[kind] + later:
                        staged(kind, j, c, stage, sig_of[c], sigs, g, gp, gq)

            for q in range(QUARTERS):
                if scan:
                    wait(act, scan_done, g * QUARTERS + (q - 1))
                    if q < 4:
                        wait(act, dt_done, g * 4 + (q + 1))
                    decay(g, q, 0, par)
                stages(q, 1, 1)
                if scan:
                    decay(g, q, 1, par)
                stages(q, 2, 1)
                stages(q, 0, 0)
                for kind, j, at, c in side:
                    if kind in ("XN", "XI", "XP", "YT") and q == at[-1] + A_AFTER[kind]:
                        simple(kind, j, c, g, gp, gq, par)
                if pre and q == Q_RSTD:
                    wait(act, stats_done, gp + 1)
                    act.activation(lnv[:, :], mv[:, :, 1], ACT.Ln, bias=C["eps"][:, 0:1]).then_inc(lnv_done, 1)
                    wait(act, lnv_done, gp + 1)
                    act.activation(rstd[:, :], lnv[:, :], ACT.Exp, scale=-0.5).then_inc(rstd_done, 1)

        over_groups(act, body)

    @block.vector
    def _(dve):
        for i in range(2):
            dve.memset(dA[i][:, :, :, 0:1], 0.0).then_inc(init_done, 1)
        dve.memset(xin[:, :, :, 0:TAPS - 1], 0.0).then_inc(init_done, 1)
        dve.memset(dtr[RANK:RANK + 1, :], 1.0).then_inc(init_done, 1)
        dve.wait_ge(init_done, 4)

        def add_c(g, half, b, par):
            n, hf = half // 2, half % 2
            idx = 2 * hf + b
            wait(dve, ht_filled, g * QUARTERS + 2 * (half + 1))
            if n == 0:
                wait(dve, acc_init, g * 4 + 4)
                wait(dve, bc_done, g + 1)
            else:
                wait(dve, c_dve, g * QUARTERS + (4 * (n - 1) + idx + 1))
            blk = acc[par][:, b, hf * D:(hf + 1) * D]
            dve.scalar_tensor_tensor(blk, hT[hf][b][:, :], ct[par][:, b, n:n + 1], blk, ALU.mult, ALU.add).then_inc(c_dve, 1)

        def side_dve(kind, j, c, sig, g, gp, gq, par):
            nxt = 1 - par
            src = bank[c % 2]
            if kind in SIGS:
                t = tmp[sig % 2]
                wait(dve, sig_ready, before(g, 8, 4) + (sig + 1))
            else:
                wait(dve, filled, before(g, N_PRE, N_POST) + (c + 1))
            if kind == "Z":
                dve.tensor_tensor(t[:, :], src[:, :], t[:, :], ALU.mult).then_inc(zs_done, 1)
            elif kind == "O":
                wait(dve, gate_loaded, gq * 16 + 16)
                dve.tensor_tensor(gb[:, j, :], src[:, :], gb[:, j, :], ALU.mult).then_inc(og_done, 1)
            elif kind == "CV":
                for e in range(2):
                    last = dve.scalar_tensor_tensor(u[nxt][:, 2 * j + e, :], src[:, e * GT:(e + 1) * GT],
                                                    C["cb"][:, 2 * j + e:2 * j + e + 1], t[:, e * GT:(e + 1) * GT],
                                                    ALU.add, ALU.mult)
                last.then_inc(u_done, 1)
            elif kind == "BC":
                wait(dve, c_dve, g * QUARTERS)
                dve.tensor_copy(ct[nxt][:, :, :], src[:, 0:GB * NST].rearrange("p (b n) -> p b n", b=GB)).then_inc(bc_done, 1)
            elif kind == "DT":
                wait(dve, dA_ready, g * QUARTERS)
                dve.scalar_tensor_tensor(dt[nxt][:, 2 * j:2 * j + 2, :].rearrange("p e t -> p (e t)"), src[:, :], 0.0, t[:, :],
                                         ALU.max, ALU.add).then_inc(dt_done, 1)
                if j % 2 == 1:
                    hf = j // 2
                    wait(dve, dt_done, gp * 4 + (j + 1))
                    for k in (4 * hf, 4 * hf + 2):
                        last = dve.tensor_tensor(u[nxt][:, k:k + 2, :], dt[nxt][:, k:k + 2, :], u[nxt][:, k:k + 2, :], ALU.mult)
                    last.then_inc(du_done, 1)
            elif kind == "UT":
                b, hf = UT_BLOCK[j]
                dve.tensor_tensor(acc[nxt][:, b, hf * D:(hf + 1) * D], src[:, :], C["dbc"][:, hf * D:(hf + 1) * D],
                                  ALU.mult).then_inc(acc_init, 1)

        def body(g, par, scan, post, pre):
            gp, gq = g + 1, g - 1
            side = side_of(post, pre)
            sig_of = {c: i for i, c in enumerate(c for kind, _, _, c in side if kind in SIGS)}
            for q in range(QUARTERS):
                if pre and q == Q_STATS + 1:
                    wait(dve, bn_done, gp * GB + GB)
                if scan:
                    wait(dve, dA_ready, g * QUARTERS + (q + 1))
                    wait(dve, dbu_ready, g * QUARTERS + (q + 1))
                    wait(dve, ht_filled, g * QUARTERS + (q + 1 - H_RING))
                    dve.tensor_tensor_scan(h[q % H_RING][:, :], dA[q % 2][:, :, :, :].rearrange("p e b t -> p (e b t)"),
                                           dbu[q % B_RING][:, :, :].rearrange("p e t -> p (e t)"), 0.0, ALU.mult, ALU.add).then_inc(scan_done, 1)
                done = sum_at(g, q, scan, post)
                if done:
                    add_c(*done, par if q >= C_LAG else 1 - par)
                if pre and q == Q_STATS:
                    wait(dve, x_loaded, gp * 16 + 16)
                    for b in range(GB):
                        dve.bn_stats(stats[:, b, :], x_in[:, b, :]).then_inc(bn_done, 1)
                if pre and q == Q_STATS + 1:
                    for b in range(GB):
                        last = dve.bn_aggr(mv[:, b, :], stats[:, b, :])
                    last.then_inc(stats_done, 1)
                if pre and q == Q_XHAT:
                    wait(dve, rstd_done, gp + 1)
                    for b in range(GB):
                        dve.tensor_scalar(xhat[:, b, :], x_in[:, b, :], mv[:, b, 0:1], rstd[:, b:b + 1],
                                          ALU.subtract, ALU.mult).then_inc(xhat_done, 1)
                for kind, j, at, c in side:
                    if kind in D_AFTER and q == at[-1] + D_AFTER[kind]:
                        side_dve(kind, j, c, sig_of.get(c), g, gp, gq, par)

        over_groups(dve, body)

    @block.gpsimd
    def _(gps):
        def scale_b(g, q, par):
            n, k = q // 4, 2 * (q % 4)
            wait(gps, scan_done, g * QUARTERS + (q + 1 - B_RING))
            if q % 16 == 0:
                wait(gps, b_loaded[q // 16], g * 16 + 16)
            if q < 4:
                wait(gps, du_done, g * 2 + (q // 2 + 1))
            gps.tensor_tensor(dbu[q % B_RING][:, :, :], u[par][:, k:k + 2, :], bbc[:, n:n + 1, :].broadcast_to([P, 2, GT]),
                              ALU.mult).then_inc(dbu_ready, 1)

        def side_gps(kind, j, sig, g, gp, gq, par):
            nxt = 1 - par
            if kind == "O":
                wait(gps, og_done, gq * GB + (j + 1))
                wait(gps, xres_loaded, gq * 16 + 16)
                gps.tensor_tensor(xres[:, j, :], xres[:, j, :], gb[:, j, :], ALU.add).then_inc(x1_done, 1)
            elif kind == "Z":
                b, hf = Z_BLOCK[j]
                wait(gps, c_dve, gq * QUARTERS + QUARTERS)
                wait(gps, zs_done, gq * 4 + (j + 1))
                blk = acc[nxt][:, b, hf * D:(hf + 1) * D]
                gps.tensor_tensor(blk, blk, tmp[sig % 2][:, :], ALU.mult).then_inc(yz_done, 1)

        def body(g, par, scan, post, pre):
            gp, gq = g + 1, g - 1
            side = side_of(post, pre)
            sig_of = {c: i for i, c in enumerate(c for kind, _, _, c in side if kind in SIGS)}
            for q in range(QUARTERS):
                if scan:
                    scale_b(g, q, par)
                for kind, j, at, c in side:
                    if kind in G_AFTER and q == at[-1] + G_AFTER[kind]:
                        side_gps(kind, j, sig_of.get(c), g, gp, gq, par)

        over_groups(gps, body)


def attention(nc, ctx, NG, C, io):

    def sb(name, shape, dt=F32):
        return ctx.enter_context(nc.sbuf_tensor("p3_" + name, shape, dt))

    def sem(name):
        return ctx.enter_context(nc.semaphore(name))

    MASKED = -3.0e38
    NH = D // HD
    wk, wv, wq, wo = (sb(n, [P, KD, D]) for n in ("wk", "wv", "wq", "wo"))
    bv, bq, bo = (sb(n, [P, D]) for n in ("bv_all", "bq_all", "bo_all"))
    cols = sb("ncols", [P, 3, KD])
    heads = sb("heads", [P, P])
    x_in = sb("x1_in", [P, GB, D])
    stats = sb("stats1", [P, GB, 6])
    mv = sb("mv1", [P, GB, 2])
    rstd = sb("rstd1", [P, 2, GB])
    xhat = sb("xhat1", [P, GB, D])
    xnF = sb("xnF1", [P, KD, GT])
    mask_i = sb("mask_i", [P, GT], I32)
    mask_f = sb("mask_f", [P, GT])
    k_e = sb("k_e", [P, KD, GT])
    kmax = sb("kmax", [P, KD, GB])
    ksum = sb("ksum", [P, KD, GB])
    v = sb("v", [P, GB, D])
    q = sb("q", [P, GB, D])
    qmax = sb("qmax", [P, GB, NH])
    qsum = sb("qsum", [P, GB, NH])
    kT = sb("kT", [P, GB, D])
    qF = sb("qF", [P, GB, KD, P])
    at = sb("at", [P, GB, KD, P])
    y = sb("y", [P, GB, D])
    yst = sb("yst", [P, GB, 6])
    ymv = sb("ymv", [P, GB, 2])
    yr = sb("yr", [P, 2, GB])
    yhat = sb("yhat", [P, GB, D])
    hp = sb("hp", [P, GB, D])
    ht = sb("ht", [P, GB, D])
    hF = sb("hF", [P, GB, D])
    xr = sb("xr", [P, GB, D])

    banks = [[ctx.enter_context(nc.psum_tensor(f"pair{i}{b}", [P, 512], F32)) for b in range(2)] for i in range(4)]

    names = ("w_in x_loaded mask_loaded xr_loaded out_stored "
             "bn_a st_a lnv_a rstd_a ln1_done xn_done mask_done k_emptied kmax_r kneg_done e_done rk_done es_done v_done "
             "q_emptied qmax_done qsub_done qe_done qsum_r rq_done kT_done qF_done at_done y_emptied bn_b st_b lnv_b rstd_b "
             "yhat_done hp_done h_step hsig_done hF_done xb_done f_done").split()
    s = {n: sem("p3_" + n) for n in names}
    f = {n: sem("p3_filled_" + n) for n in ("XN", "K", "V", "Q", "ET", "QT", "AT", "Y", "HT", "F")}

    def over_groups(eng, body):
        def peeled(g):
            body(g, g + 2 < NG, 0 <= g + 1 < NG, 0 <= g < NG, 0 <= g - 1)

        for g in range(-2, 2):
            peeled(g)
        with eng.Fori(0, NG - 4) as i:
            body(i + 2, True, True, True, True)
        for g in range(NG - 2, NG + 1):
            peeled(g)

    block = ctx.enter_context(nc.Block())

    @block.sync
    def _(sp):
        def load_weights():
            for w, name in ((wk, "Wk"), (wv, "Wv"), (wq, "Wq"), (wo, "Wo")):
                sp.dma_start(w[:, :, :], io[name].rearrange("(k p) n -> p k n", p=P)).then_inc(s["w_in"], 16)
            for t, name in ((bv, "bv"), (bq, "bq"), (bo, "bo")):
                sp.dma_start(t[:, :], io[name].partition_broadcast(P)).then_inc(s["w_in"], 16)
            for n, name in enumerate(("n_g", "n_b", "bk")):
                sp.dma_start(cols[:, n, :], io[name]).then_inc(s["w_in"], 16)
            sp.dma_start(heads[:, :], io["heads"]).then_inc(s["w_in"], 16)

        def body(g, S, A, B, Cc):
            sg, a, c = g + 2, g + 1, g - 1
            if S:
                sp_wait(sp, s["ln1_done"], sg * GB)
                sp.dma_start(x_in[:, :, :], io["x1"][bass.ds(sg * GB, GB), :, :].rearrange("b t d -> t b d")).then_inc(s["x_loaded"], 16)
            if isinstance(g, int) and g == -2:
                load_weights()
            if A:
                sp_wait(sp, s["mask_done"], a)
                sp.dma_start(mask_i[:, :].rearrange("p (b t) -> p b t", b=GB),
                             io["mask"][bass.ds(a * GB, GB), :].partition_broadcast(P)).then_inc(s["mask_loaded"], 16)
            if Cc:
                sp_wait(sp, s["out_stored"], c * 16)
                sp.dma_start(xr[:, :, :], io["x1"][bass.ds(c * GB, GB), :, :].rearrange("b t d -> t b d")).then_inc(s["xr_loaded"], 16)
                sp_wait(sp, s["f_done"], c * GB + GB)
                sp.dma_start(io["out"][bass.ds(c * GB, GB), :, :].rearrange("b t d -> t b d"), xr[:, :, :]).then_inc(s["out_stored"], 16)

        over_groups(sp, body)
        sp.wait_ge(s["out_stored"], 16 * NG)

    @block.tensor
    def _(pe):
        ident = C["ident"][:, :]

        def turn(out, src):
            for k in range(KD):
                last = pe.transpose(out[:, k * P:(k + 1) * P], src[:, k * P:(k + 1) * P], ident)
            return last

        def product(out, lhs, w):
            for k in range(KD):
                last = pe.matmul(out[:, :], lhs(k), w[:, k, :], start=(k == 0), stop=(k == KD - 1))
            return last

        def body(g, S, A, B, Cc):
            a, c = g + 1, g - 1
            if B:
                for b in range(GB):
                    wait(pe, s["es_done"], g * 2 + 2)
                    wait(pe, s["f_done"], g * 2 + (b - 3))
                    for k in range(KD):
                        last = pe.transpose(banks[0][b][:, k * P:(k + 1) * P], k_e[:, k, b * P:(b + 1) * P], ident)
                    last.then_inc(f["ET"], 1)
            if A:
                for j in range(2):
                    wait(pe, s["ln1_done"], a * 2 + 2)
                    wait(pe, s["q_emptied"], a * 2 + (j - 1))
                    for e in range(2):
                        for b in range(GB):
                            o, k = (e * GB + b) * P, 2 * j + e
                            last = pe.transpose(banks[1][j][:, o:o + P], xhat[:, b, k * P:(k + 1) * P], ident)
                    last.then_inc(f["XN"], 1)
            if B:
                for b in range(GB):
                    wait(pe, s["kT_done"], g * 2 + (b + 1))
                    wait(pe, s["v_done"], g * 2 + (b + 1))
                    wait(pe, s["y_emptied"], g * 2 + (b - 1))
                    for k in range(KD):
                        last = pe.matmul(banks[3][b][:, k * P:(k + 1) * P], v[:, b, k * P:(k + 1) * P],
                                         kT[:, b, k * P:(k + 1) * P], start=True, stop=True)
                    last.then_inc(f["AT"], 1)
            if Cc:
                for b in range(GB):
                    wait(pe, s["yhat_done"], c * 2 + (b + 1))
                    if B:
                        wait(pe, s["kT_done"], g * 2 + (b + 1))
                    wait(pe, s["f_done"], c * 2 + (b - 1))
                    turn(banks[0][b], yhat[:, b, :]).then_inc(f["HT"], 1)
            if A:
                if isinstance(g, int) and g == -1:
                    pe.wait_ge(s["w_in"], 16 * 11)
                for j in range(2):
                    wait(pe, s["xn_done"], a * 2 + 2)
                    for e in range(2):
                        for k in range(KD):
                            m = (2 * j + e) * P
                            last = pe.matmul(banks[1][j][:, e * GT:(e + 1) * GT], wk[:, k, m:m + P], xnF[:, k, :],
                                             start=(k == 0), stop=(k == KD - 1))
                    last.then_inc(f["K"], 1)
            if B:
                for b in range(GB):
                    wait(pe, s["qe_done"], g * 2 + (b + 1))
                    wait(pe, s["v_done"], g * 2 + (b + 1))
                    turn(banks[2][b], q[:, b, :]).then_inc(f["QT"], 1)

            def values(b):
                wait(pe, s["qF_done"], a * 2 + (b - 1))
                product(banks[2][b], lambda k: xnF[:, k, b * P:(b + 1) * P], wv).then_inc(f["V"], 1)

            def queries(b):
                wait(pe, s["k_emptied"], a * 2 + (b + 1))
                product(banks[1][b], lambda k: xnF[:, k, b * P:(b + 1) * P], wq).then_inc(f["Q"], 1)

            def film_product(b):
                wait(pe, s["hF_done"], c * 2 + (b + 1))
                product(banks[0][b], lambda k: hF[:, b, k * P:(k + 1) * P], wo).then_inc(f["F"], 1)

            if A:
                values(0)
            if B:
                for b in range(GB):
                    wait(pe, s["at_done"], g * 2 + (b + 1))
                    wait(pe, s["qF_done"], g * 2 + (b + 1))
                    for k in range(KD):
                        last = pe.matmul(banks[3][b][:, k * P:(k + 1) * P], qF[:, b, k, :], at[:, b, k, :], start=True, stop=True)
                    last.then_inc(f["Y"], 1)
            if A:
                values(1)
            if Cc:
                film_product(0)
            if A:
                queries(0)
            if Cc:
                film_product(1)
            if A:
                queries(1)

        over_groups(pe, body)

    @block.scalar
    def _(act):
        act.preload_act_table_set("natural_log_exp_and_others")

        def body(g, S, A, B, Cc):
            sg, a, c = g + 2, g + 1, g - 1
            if B:
                for b in range(GB):
                    wait(act, f["ET"], g * 2 + (b + 1))
                    act.activation(kT[:, b, :], banks[0][b][:, :], ACT.Copy).then_inc(s["kT_done"], 1)
            if A:
                if isinstance(g, int) and g == -1:
                    act.wait_ge(s["w_in"], 16 * 11)
                for j in range(2):
                    wait(act, f["XN"], a * 2 + (j + 1))
                    wait(act, f["Q"], a * 2)
                    for e in range(2):
                        k = 2 * j + e
                        last = act.activation(xnF[:, k, :], banks[1][j][:, e * GT:(e + 1) * GT], ACT.Identity,
                                              scale=cols[:, 0, k:k + 1], bias=cols[:, 1, k:k + 1])
                    last.then_inc(s["xn_done"], 1)
            if Cc:
                for b in range(GB):
                    wait(act, s["hp_done"], c * 2 + (b + 1))
                    wait(act, s["hF_done"], c * 2 + (b - 1))
                    act.activation(ht[:, b, :], hp[:, b, :], ACT.Exp, scale=-1.0).then_inc(s["h_step"], 1)
                for b in range(GB):
                    wait(act, s["h_step"], c * 4 + (b + 1))
                    act.activation(ht[:, b, :], ht[:, b, :], ACT.Ln, bias=1.0).then_inc(s["h_step"], 1)
                for b in range(GB):
                    wait(act, s["h_step"], c * 4 + (b + 3))
                    act.activation(ht[:, b, :], ht[:, b, :], ACT.Exp, scale=-1.0).then_inc(s["hsig_done"], 1)
            if B:
                for b in range(GB):
                    wait(act, f["QT"], g * 2 + (b + 1))
                    act.activation(qF[:, b, :, :].rearrange("p k t -> p (k t)"), banks[2][b][:, :], ACT.Copy).then_inc(s["qF_done"], 1)
            if A:
                for j in range(2):
                    wait(act, s["kneg_done"], a * 2 + (j + 1))
                    for e in range(2):
                        for b in range(GB):
                            k = 2 * j + e
                            blk = k_e[:, k, b * P:(b + 1) * P]
                            last = act.activation(blk, blk, ACT.Exp, bias=kmax[:, k, b:b + 1], accum_out=ksum[:, k, b:b + 1])
                    last.then_inc(s["e_done"], 1)
            if S:
                wait(act, s["st_a"], sg + 1)
                act.activation(rstd[:, 0, :], mv[:, :, 1], ACT.Ln, bias=C["eps"][:, 0:1]).then_inc(s["lnv_a"], 1)
                wait(act, s["lnv_a"], sg + 1)
                act.activation(rstd[:, 1, :], rstd[:, 0, :], ACT.Exp, scale=-0.5).then_inc(s["rstd_a"], 1)
            if B:
                for b in range(GB):
                    wait(act, s["st_b"], g * 2 + (b + 1))
                    act.activation(yr[:, 0, b:b + 1], ymv[:, b, 1:2], ACT.Ln, bias=C["eps"][:, 0:1]).then_inc(s["lnv_b"], 1)
                for b in range(GB):
                    wait(act, s["lnv_b"], g * 2 + (b + 1))
                    act.activation(yr[:, 1, b:b + 1], yr[:, 0, b:b + 1], ACT.Exp, scale=-0.5).then_inc(s["rstd_b"], 1)
            if A:
                for b in range(GB):
                    wait(act, s["qsub_done"], a * 2 + (b + 1))
                    act.activation(q[:, b, :], q[:, b, :], ACT.Exp).then_inc(s["qe_done"], 1)

        over_groups(act, body)

    @block.vector
    def _(dve):
        def by_head(t):
            return t.rearrange("p (h e) -> p h e", e=HD)

        def body(g, S, A, B, Cc):
            sg, a, c = g + 2, g + 1, g - 1
            if isinstance(g, int) and g == -1:
                dve.wait_ge(s["w_in"], 16 * 11)
            if A:
                wait(dve, s["mask_loaded"], a * 16 + 16)
                dve.tensor_scalar(mask_f[:, :], mask_i[:, :], 1.0, MASKED, ALU.is_equal, ALU.mult).then_inc(s["mask_done"], 1)
            if B:
                for b in range(GB):
                    wait(dve, f["AT"], g * 2 + (b + 1))
                    dve.tensor_tensor(at[:, b, :, :], banks[3][b][:, :].rearrange("p (k e) -> p k e", k=KD),
                                      heads[:, :].unsqueeze(1).broadcast_to([P, KD, P]), ALU.mult).then_inc(s["at_done"], 1)
            if Cc:
                for b in range(GB):
                    wait(dve, f["HT"], c * 2 + (b + 1))
                    wait(dve, s["hF_done"], c * 2 + (b - 1))
                    for k in range(KD):
                        last = dve.tensor_scalar(hp[:, b, k * P:(k + 1) * P], banks[0][b][:, k * P:(k + 1) * P],
                                                 C["gm1"][:, bass.ds(c * GB + b, 1), k], C["bm1"][:, bass.ds(c * GB + b, 1), k],
                                                 ALU.mult, ALU.add)
                    last.then_inc(s["hp_done"], 1)
            if A:
                wait(dve, s["mask_done"], a + 1)
                for j in range(2):
                    wait(dve, f["K"], a * 2 + (j + 1))
                    wait(dve, f["ET"], a * 2)
                    for e in range(2):
                        k = 2 * j + e
                        last = dve.scalar_tensor_tensor(k_e[:, k, :], banks[1][j][:, e * GT:(e + 1) * GT], cols[:, 2, k:k + 1],
                                                        mask_f[:, :], ALU.add, ALU.add)
                    last.then_inc(s["k_emptied"], 1)
                    wait(dve, s["k_emptied"], a * 2 + (j + 1))
                    km = kmax[:, 2 * j:2 * j + 2, :].rearrange("p k b -> p (k b)")
                    dve.tensor_reduce(km, k_e[:, 2 * j:2 * j + 2, :].rearrange("p k (b t) -> p (k b) t", b=GB), AX.X,
                                      ALU.max).then_inc(s["kmax_r"], 1)
                    wait(dve, s["kmax_r"], a * 2 + (j + 1))
                    dve.tensor_scalar(km, km, -1.0, None, ALU.mult).then_inc(s["kneg_done"], 1)

            def values(b):
                wait(dve, f["V"], a * 2 + (b + 1))
                dve.tensor_tensor(v[:, b, :], banks[2][b][:, :], bv[:, :], ALU.add).then_inc(s["v_done"], 1)

            if S:
                wait(dve, s["x_loaded"], sg * 16 + 16)
                for b in range(GB):
                    dve.bn_stats(stats[:, b, :], x_in[:, b, :]).then_inc(s["bn_a"], 1)
                wait(dve, s["bn_a"], sg * 2 + 2)
            if A:
                values(0)
            if S:
                for b in range(GB):
                    last = dve.bn_aggr(mv[:, b, :], stats[:, b, :])
                last.then_inc(s["st_a"], 1)
            if B:
                for b in range(GB):
                    wait(dve, f["Y"], g * 2 + (b + 1))
                    wait(dve, s["rq_done"], g * 2 + (b + 1))
                    dve.tensor_tensor(by_head(y[:, b, :]), by_head(banks[3][b][:, :]),
                                      qsum[:, b, :].unsqueeze(2).broadcast_to([P, NH, HD]), ALU.mult).then_inc(s["y_emptied"], 1)
                    wait(dve, s["y_emptied"], g * 2 + (b + 1))
                    dve.bn_stats(yst[:, b, :], y[:, b, :]).then_inc(s["bn_b"], 1)
            if B:
                wait(dve, s["bn_b"], g * 2 + 2)
            if A:
                values(1)
            if B:
                for b in range(GB):
                    dve.bn_aggr(ymv[:, b, :], yst[:, b, :]).then_inc(s["st_b"], 1)
            if A:
                wait(dve, s["e_done"], a * 2 + 2)
                dve.reciprocal(ksum[:, :, :], ksum[:, :, :]).then_inc(s["rk_done"], 1)
            if B:
                wait(dve, f["HT"], g * 2)
                for b in range(GB):
                    wait(dve, s["rstd_b"], g * 2 + (b + 1))
                    dve.tensor_scalar(yhat[:, b, :], y[:, b, :], ymv[:, b, 0:1], yr[:, 1, b:b + 1], ALU.subtract,
                                      ALU.mult).then_inc(s["yhat_done"], 1)

            if S:
                wait(dve, f["XN"], sg * 2)
                wait(dve, s["rstd_a"], sg + 1)
                for b in range(GB):
                    dve.tensor_scalar(xhat[:, b, :], x_in[:, b, :], mv[:, b, 0:1], rstd[:, 1, b:b + 1], ALU.subtract,
                                      ALU.mult).then_inc(s["ln1_done"], 1)

            def result(b):
                wait(dve, f["F"], c * 2 + (b + 1))
                wait(dve, s["xb_done"], c * 2 + (b + 1))
                dve.tensor_tensor(xr[:, b, :], banks[0][b][:, :], xr[:, b, :], ALU.add).then_inc(s["f_done"], 1)

            def queries(b):
                wait(dve, f["Q"], a * 2 + (b + 1))
                dve.tensor_tensor(q[:, b, :], banks[1][b][:, :], bq[:, :], ALU.add).then_inc(s["q_emptied"], 1)
                wait(dve, s["q_emptied"], a * 2 + (b + 1))
                dve.tensor_reduce(qmax[:, b, :], by_head(q[:, b, :]), AX.X, ALU.max).then_inc(s["qmax_done"], 1)

            if Cc:
                result(0)
            if A:
                queries(0)
            if Cc:
                result(1)
            if A:
                queries(1)
            def sum_queries(b):
                wait(dve, s["qe_done"], a * 2 + (b + 1))
                dve.tensor_reduce(qsum[:, b, :], by_head(q[:, b, :]), AX.X, ALU.add).then_inc(s["qsum_r"], 1)

            if A:
                sum_queries(0)
                sum_queries(1)
                for b in range(GB):
                    wait(dve, s["qsum_r"], a * 2 + (b + 1))
                    dve.reciprocal(qsum[:, b, :], qsum[:, b, :]).then_inc(s["rq_done"], 1)

        over_groups(dve, body)

    @block.gpsimd
    def _(gps):
        gps.wait_ge(s["w_in"], 16 * 11)

        def body(g, S, A, B, Cc):
            a, c = g + 1, g - 1
            if Cc:
                wait(gps, s["xr_loaded"], c * 16 + 16)
                for b in range(GB):
                    gps.tensor_tensor(xr[:, b, :], xr[:, b, :], bo[:, :], ALU.add).then_inc(s["xb_done"], 1)
                for b in range(GB):
                    wait(gps, s["hsig_done"], c * 2 + (b + 1))
                    wait(gps, f["F"], c * 2 + (b - 1))
                    gps.tensor_tensor(hF[:, b, :], hp[:, b, :], ht[:, b, :], ALU.mult).then_inc(s["hF_done"], 1)
            if A:
                for j in range(2):
                    wait(gps, s["rk_done"], a + 1)
                    blk = k_e[:, 2 * j:2 * j + 2, :].rearrange("p k (b t) -> p (k b) t", b=GB)
                    r = ksum[:, 2 * j:2 * j + 2, :].rearrange("p k b -> p (k b)").unsqueeze(2).broadcast_to([P, 4, P])
                    gps.tensor_tensor(blk, blk, r, ALU.mult).then_inc(s["es_done"], 1)
                for b in range(GB):
                    wait(gps, s["qmax_done"], a * 2 + (b + 1))
                    blk = q[:, b, :].rearrange("p (h e) -> p h e", e=HD)
                    gps.tensor_tensor(blk, blk, qmax[:, b, :].unsqueeze(2).broadcast_to([P, NH, HD]), ALU.subtract).then_inc(s["qsub_done"], 1)

        over_groups(gps, body)


def setup(nc, ctx, NB, W, C, io):

    def sb(name, shape, dt=F32):
        return ctx.enter_context(nc.sbuf_tensor(name, shape, dt))

    def sem(name):
        return ctx.enter_context(nc.semaphore(name))

    KC = COND // P
    cT = sb("cT", [P, KC, NB])
    ec = sb("ec", [P, KC, NB])
    ada = sb("ada", [P, KC, 3 * D])
    film = sb("film", [P, KC, 2 * D])
    cols = sb("cols", [P, 9, KD])
    one_plus = sb("one_plus", [P, 2, KD])
    t0 = sb("t0", [P, 2, KD, NB])
    gbias = sb("gbias", [NB, D])
    gate = sb("gate", [NB, D])
    mod = sb("mod", [P, 4, D])
    ps = [ctx.enter_context(nc.psum_tensor(f"mod{i}", [P, 512], F32)) for i in range(8)]
    turned = [ps[5], ps[6], ps[7], ps[0]]

    cond_in, early_in, cols_in, gbias_in, weights_in, gate_out = (
        sem(n) for n in ("cond_in", "early_in", "cols_in", "gbias_in", "weights_in", "gate_out"))
    mats_in = [sem(f"mats_in{k}") for k in range(KC)]
    cleared, mod_copied, mod_turned = (sem(n) for n in ("cleared", "mod_copied", "mod_turned"))
    silu_e, silu_v, mod_done, mod_v, gate_v, a_exp = (sem(n) for n in ("silu_e", "silu_v", "mod_done", "mod_v", "gate_v", "a_exp"))
    LN_G, LN_B, SHIFT, SCALE, F_SCALE, F_SHIFT, F_G, F_B = range(8)

    block = ctx.enter_context(nc.Block())

    @block.sync
    def _(sp):
        sp.dma_start(cT[:, :, :], io["condT"].rearrange("(k p) b -> p k b", p=P)).then_inc(cond_in, 16)
        ada_v = io["adaT"].rearrange("(k p) n -> p k n", p=P)
        film_v = io["filmW"].rearrange("(k p) n -> p k n", p=P)
        sp.dma_start(C["ident"][:, :], io["ident"]).then_inc(early_in, 16)
        sp.dma_start(C["cw"][:, :, :], io["conv_w"]).then_inc(early_in, 16)
        for k in range(KC):
            sp.dma_start(ada[:, k, :], ada_v[:, k, :]).then_inc(mats_in[k], 16)
            sp.dma_start(film[:, k, :], film_v[:, k, :]).then_inc(mats_in[k], 16)
        for i, name in enumerate(("ln_g", "ln_b", "b_shift", "b_scale", "bf_scale", "bf_shift", "fn_g", "fn_b")):
            sp.dma_start(cols[:, i, :], io[name]).then_inc(cols_in, 16)
        sp.dma_start(gbias[:, :], io["b_gate"].partition_broadcast(NB)).then_inc(gbias_in, 16)
        sp.dma_start(C["cb"][:, :], io["conv_b"]).then_inc(weights_in, 16)
        sp.dma_start(C["A"][:, :, :], io["A_log"].rearrange("(k p) n -> p k n", p=P)).then_inc(weights_in, 16)
        sp.dma_start(C["dbc"][:, :], io["D"].partition_broadcast(P)).then_inc(weights_in, 16)
        sp.dma_start(W["dt"][0:RANK, :], io["dtT"]).then_inc(weights_in, 16)
        sp.dma_start(W["dt"][RANK:RANK + 1, :], io["dt_b"]).then_inc(weights_in, 16)
        sp.dma_start(W["x"][:, :, :], io["xT"].rearrange("(k p) n -> p k n", p=P)).then_inc(weights_in, 16)
        for k in range(KD):
            sp.dma_start(W["in"][:, k, :], io["inT"].rearrange("(k p) n -> p k n", p=P)[:, k, :]).then_inc(weights_in, 16)
        sp.dma_start(W["out"][:, :, :], io["outT"].rearrange("(k p) n -> p k n", p=P)).then_inc(weights_in, 16)
        sp.wait_ge(weights_in, 16 * (7 + KD))
        sp.wait_ge(gate_v, 1)
        sp.dma_start(io["gate"], gate[:, :]).then_inc(gate_out, 16)
        sp.wait_ge(gate_out, 16)

    @block.scalar
    def _(act):
        act.preload_act_table_set("natural_log_exp_and_others")
        act.wait_ge(cond_in, 16)
        act.activation(ec[:, :, :], cT[:, :, :], ACT.Exp, scale=-1.0).then_inc(silu_e, 1)
        act.wait_ge(weights_in, 16 * (7 + KD))
        act.activation(C["A"][:, :, :], C["A"][:, :, :], ACT.Exp).then_inc(a_exp, 1)

    @block.tensor
    def _(pe):
        pe.wait_ge(silu_v, 3)
        for c in range(KC):
            pe.wait_ge(mats_in[c], 32)
            for i, (m, off) in enumerate(((ada, 0), (ada, D), (film, 0), (film, D), (ada, 2 * D))):
                last = pe.matmul(ps[i][0:NB, :], cT[:, c, :], m[:, c, off:off + D], start=(c == 0), stop=(c == KC - 1))
        last.then_inc(mod_done, 1)
        pe.wait_ge(early_in, 32)
        for i in range(4):
            pe.wait_ge(mod_copied, i + 1)
            for k in range(KD):
                last = pe.transpose(turned[i][:, k * P:(k + 1) * P], mod[:, i, k * P:(k + 1) * P], C["ident"][:, :])
        last.then_inc(mod_turned, 1)

    @block.vector
    def _(dve):
        dve.wait_ge(silu_e, 1)
        dve.tensor_scalar(ec[:, :, :], ec[:, :, :], 1.0, None, ALU.add).then_inc(silu_v, 1)
        dve.wait_ge(silu_v, 1)
        dve.reciprocal(ec[:, :, :], ec[:, :, :]).then_inc(silu_v, 1)
        dve.wait_ge(silu_v, 2)
        dve.tensor_tensor(cT[:, :, :], cT[:, :, :], ec[:, :, :], ALU.mult).then_inc(silu_v, 1)
        dve.wait_ge(early_in, 32)
        for e in range(KI):
            for t in range(TAPS):
                dve.tensor_scalar(W["conv"][:, e, t, :], C["ident"][:, :], C["cw"][:, e, t:t + 1], None, ALU.mult)
        dve.wait_ge(cols_in, 16 * 8)
        dve.tensor_scalar(one_plus[:, 0, :], cols[:, SCALE, :], 1.0, None, ALU.add).then_inc(mod_v, 1)
        dve.tensor_scalar(one_plus[:, 1, :], cols[:, F_SCALE, :], 1.0, None, ALU.add).then_inc(mod_v, 1)
        dve.wait_ge(cleared, 1)
        dve.wait_ge(mod_done, 1)
        for i in range(4):
            dve.tensor_copy(mod[0:NB, i, :], ps[i][0:NB, :]).then_inc(mod_copied, 1)
        dve.wait_ge(gbias_in, 16)
        dve.tensor_tensor(gate[:, :], ps[4][0:NB, :], gbias[:, :], ALU.add).then_inc(gate_v, 1)
        dve.wait_ge(mod_v, 2)
        dve.wait_ge(mod_turned, 1)
        for i, (scale, shift, g, b, gm, bm) in enumerate(((1, 0, LN_G, LN_B, "gm0", "bm0"), (2, 3, F_G, F_B, "gm1", "bm1"))):
            for k in range(KD):
                sc = turned[scale][:, k * P:k * P + NB]
                dve.tensor_scalar(C[gm][:, :, k], sc, one_plus[:, i, k:k + 1], cols[:, g, k:k + 1], ALU.add, ALU.mult)
                dve.tensor_scalar(t0[:, i, k, :], sc, one_plus[:, i, k:k + 1], cols[:, b, k:k + 1], ALU.add,
                                  ALU.mult).then_inc(mod_v, 1)
        dve.wait_ge(mod_v, 2 + 2 * KD)
        for i, (shift, bias, bm) in enumerate(((0, SHIFT, "bm0"), (3, F_SHIFT, "bm1"))):
            for k in range(KD):
                dve.scalar_tensor_tensor(C[bm][:, :, k], turned[shift][:, k * P:k * P + NB], cols[:, bias, k:k + 1],
                                         t0[:, i, k, :], ALU.add, ALU.add)
        dve.wait_ge(weights_in, 16 * (7 + KD))
        dve.tensor_scalar(C["ncb"][:, :], C["cb"][:, :], -1.0, None, ALU.mult)
        dve.memset(C["eps"][:, :], EPS)
        dve.wait_ge(a_exp, 1)
        dve.tensor_scalar(C["A"][:, :, :], C["A"][:, :, :], -1.0, None, ALU.mult)

    @block.gpsimd
    def _(gps):
        gps.memset(mod[:, :, :], 0.0).then_inc(cleared, 1)


def program(nc, io, NB):
    NG = NB // GB
    with ExitStack() as all_parts:
        def const(stack, where, name, shape):
            where[name] = stack.enter_context(nc.sbuf_tensor("c_" + name, shape, F32))

        C, W = {}, {}
        for name, shape in (("ident", [P, P]), ("gm0", [P, NB, KD]), ("bm0", [P, NB, KD]), ("gm1", [P, NB, KD]), ("bm1", [P, NB, KD]),
                            ("eps", [P, 1])):
            const(all_parts, C, name, shape)
        with ExitStack() as layer0:
            for name, shape in (("A", [P, KI, NST]), ("cw", [P, KI, TAPS]), ("cb", [P, KI]), ("ncb", [P, KI]), ("dbc", [P, DI])):
                const(layer0, C, name, shape)
            for name, shape in (("in", [P, KD, 2 * DI]), ("x", [P, KI, RANK + 2 * NST]), ("dt", [RANK + 1, DI]),
                                ("out", [P, KI, D]), ("conv", [P, KI, TAPS, P])):
                const(layer0, W, name + "_w", shape)
                W[name] = W[name + "_w"]
            with ExitStack() as ctx:
                setup(nc, ctx, NB, W, C, io)
            with ExitStack() as ctx:
                mamba(nc, ctx, NG, W, C, io)
        with ExitStack() as ctx:
            attention(nc, ctx, NG, C, io)


def arrays_of(inputs):
    import numpy as np

    def T(a):
        return np.ascontiguousarray(np.asarray(a).T)

    def col(v):
        v = np.asarray(v)
        return np.ascontiguousarray(v.reshape(-1, P).T)

    i = {k: np.asarray(v) for k, v in inputs.items()}
    L0, L1 = "L0_cond_", "L1_cond_"
    ada_b, film_b = i[L0 + "ada_b"], i[L1 + "film_emb_b"]
    heads = np.kron(np.eye(P // HD, dtype=np.float32), np.ones((HD, HD), np.float32))
    return {
        "x": i["x"], "condT": T(i["cond_2048"]), "mask": i["mask_BxS_ik0"],
        "adaT": T(i[L0 + "ada_w"]), "filmW": i[L1 + "film_emb_W"],
        "ln_g": col(i[L0 + "ln_g"]), "ln_b": col(i[L0 + "ln_b"]),
        "b_shift": col(ada_b[:D]), "b_scale": col(ada_b[D:2 * D]), "b_gate": ada_b[2 * D:].copy(),
        "bf_scale": col(film_b[:D]), "bf_shift": col(film_b[D:]),
        "fn_g": col(i[L1 + "film_norm_scale"]), "fn_b": col(i[L1 + "film_norm_bias"]),
        "ident": np.eye(P, dtype=np.float32), "heads": heads,
        "conv_w": np.ascontiguousarray(i[L0 + "conv_w"].reshape(KI, P, TAPS).transpose(1, 0, 2)), "conv_b": col(i[L0 + "conv_b"]),
        "A_log": i[L0 + "A_log"], "D": i[L0 + "D_param"],
        "dtT": T(i[L0 + "dt_proj_w"]), "dt_b": i[L0 + "dt_proj_b"].reshape(1, DI), "xT": T(i[L0 + "x_proj_w"]),
        "inT": T(i[L0 + "in_proj_w"]), "outT": T(i[L0 + "out_proj_w"]),
        "n_g": col(i[L1 + "norm_scale"]), "n_b": col(i[L1 + "norm_bias"]),
        "Wq": i[L1 + "Wq"], "Wk": i[L1 + "Wk"], "Wv": i[L1 + "Wv"], "Wo": i[L1 + "film_out_W"],
        "bq": i[L1 + "bq"], "bk": col(i[L1 + "bk"]), "bv": i[L1 + "bv"], "bo": i[L1 + "film_out_b"],
    }


def kernel(**inputs):
    import numpy as _np
    import concourse.bacc as _bacc
    from concourse import mybir as _mybir
    from concourse.bass_utils import run_bass_kernel_spmd as _run

    nc = _bacc.Bacc("TRN2", target_bir_lowering=False, num_devices=1)
    arrays = {f"in_{k}": _np.ascontiguousarray(v) for k, v in arrays_of(inputs).items()}
    NB = arrays["in_x"].shape[0]
    io = {k[3:]: nc.dram_tensor(k, v.shape, _mybir.dt.from_np(v.dtype), kind="ExternalInput").ap() for k, v in arrays.items()}
    io["gate"] = nc.dram_tensor("gate_scratch", (NB, D), F32, kind="Internal").ap()
    io["b"] = nc.dram_tensor("b_scratch", (NST, GT), F32, kind="Internal").ap()
    io["x1"] = nc.dram_tensor("x1_scratch", (NB, P, D), F32, kind="Internal").ap()
    io["out"] = nc.dram_tensor("out_0", (NB, P, D), F32, kind="ExternalOutput").ap()
    program(nc, io, NB)
    r = _run(nc, [arrays], core_ids=[0])
    return r.results[0]["out_0"]
```
